# Optimizing a Trainium2 kernel written in Bass

```python
import numpy as np
import jax
import jax.numpy as jnp

def _softmax(x, axis=-1):
    return jax.nn.softmax(x, axis=axis)

def _gelu(x):
    return jax.nn.gelu(x, approximate=True)

def _silu(x):
    return jax.nn.silu(x)

def _sigmoid(x):
    return jax.nn.sigmoid(x)

def _layernorm(x, axis=-1, eps=1e-05):
    m = jnp.mean(x, axis=axis, keepdims=True)
    v = jnp.var(x, axis=axis, keepdims=True)
    return (x - m) / jnp.sqrt(v + eps)

def _scatter_add(tgt, idx, src, axis=0):
    return tgt.at[idx].add(src)

def _segment_sum(src, seg, n):
    return jax.ops.segment_sum(src, seg, n)
kernel_name = 'mk_flamingo_gated_d1_seqx_r8_465a3d'

def setup_inputs(seed: int=0):
    np.random.seed(seed)
    _w = jnp.asarray

    def _rec_inputs():
        import jax
        import jax.numpy as jnp
        _rk = jax.random.key(seed)
        x = 4.136e-05 + 0.9999 * jax.random.normal(jax.random.fold_in(_rk, 1), (4, 256, 256), jnp.float32)
        _lenS = 256 - jax.random.randint(jax.random.fold_in(_rk, 7), (4,), 0, max(1, 256 // 4) + 1, jnp.int32)
        _lenS2 = 256 - jax.random.randint(jax.random.fold_in(_rk, 8), (4,), 0, max(1, 256 // 4) + 1, jnp.int32)
        _ctx_1024P = jax.random.normal(jax.random.fold_in(_rk, 11), (4, 16, 128), jnp.float32)
        _ctx_1024c = jax.random.dirichlet(jax.random.fold_in(_rk, 511), 0.3 * jnp.ones((16,), jnp.float32), (4, 256))
        _ctx_1024t = jnp.einsum('bsk,bkd->bsd', _ctx_1024c, _ctx_1024P)
        _ctx_1024t = _ctx_1024t * jax.lax.rsqrt(jnp.mean(jnp.square(_ctx_1024t)) + 1e-12) * 0.953939
        ctx_1024 = -0.000292821 + 1.00034 * (_ctx_1024t + 0.3 * jax.random.normal(jax.random.fold_in(_rk, 611), (4, 256, 128), jnp.float32))
        _g = jax.random.normal(jax.random.fold_in(_rk, 9001), (2, 1), jnp.float32)
        _g = jnp.sign(_g) * jnp.maximum(jnp.abs(_g), 1.0) + (_g == 0) * 1.0
        g_xattn = _g[0]
        g_ffn = _g[1]
        return (x, ctx_1024, g_xattn, g_ffn)
    x, ctx_1024, g_xattn, g_ffn = _rec_inputs()

    def _L0_xattn_setup():
        import jax, jax.numpy as jnp
        import numpy as np
        import math
        B, L, DM = (2, 256, 128)
        DS, DC, EXP = (16, 4, 2)
        DI = EXP * DM
        DR = math.ceil(DM / 16)
        DT_MIN, DT_MAX, DT_FLOOR = (0.001, 0.1, 0.0001)

        def _ssm_forward(hidden_states, z, in_proj_w, conv_w, conv_b, x_proj_w, dt_proj_w, dt_proj_b, A_log, D):
            b = hidden_states.shape[0]
            x = jnp.einsum('ed,bld->bel', in_proj_w, hidden_states)
            xp = jnp.pad(x, ((0, 0), (0, 0), (DC - 1, 0)))
            xc = jax.lax.conv_general_dilated(xp, conv_w[:, None, :], window_strides=(1,), padding='VALID', dimension_numbers=('NCH', 'OIH', 'NCH'), feature_group_count=DI)
            u = jax.nn.silu(xc + conv_b[None, :, None])
            x_dbl = jnp.einsum('ke,bel->bkl', x_proj_w, u)
            dt_lo = x_dbl[:, :DR]
            Bm = x_dbl[:, DR:DR + DS]
            Cm = x_dbl[:, DR + DS:]
            delta = jax.nn.softplus(jnp.einsum('er,brl->bel', dt_proj_w, dt_lo) + dt_proj_b[None, :, None])
            A = -jnp.exp(A_log)

            def step(state, xs):
                d_t, B_t, C_t, u_t = xs
                dA = jnp.exp(d_t[..., None] * A)
                state = state * dA + (d_t * u_t)[..., None] * B_t[:, None, :]
                y_t = jnp.einsum('ben,bn->be', state, C_t)
                return (state, y_t)
            xs = (jnp.moveaxis(delta, -1, 0), jnp.moveaxis(Bm, -1, 0), jnp.moveaxis(Cm, -1, 0), jnp.moveaxis(u, -1, 0))
            state0 = jnp.zeros((b, DI, DS), delta.dtype)
            _, ys = jax.lax.scan(step, state0, xs)
            y = jnp.moveaxis(ys, 0, -1)
            y = y + D[None, :, None] * u
            y = y * jax.nn.silu(z)
            return jnp.swapaxes(y, 1, 2)
        key = jax.random.key(seed)
        ks = jax.random.split(key, 8)
        hidden_states = jax.random.normal(ks[0], (B, L, DM), jnp.float32)
        z = jax.random.normal(ks[1], (B, DI, L), jnp.float32)
        in_proj_w = jax.random.normal(ks[2], (DI, DM), jnp.float32) * DM ** (-0.5)
        conv_w = jax.random.normal(ks[3], (DI, DC), jnp.float32) * DC ** (-0.5)
        conv_b = jnp.zeros((DI,), jnp.float32)
        x_proj_w = jax.random.normal(ks[4], (DR + 2 * DS, DI), jnp.float32) * DI ** (-0.5)
        dt_std = DR ** (-0.5)
        dt_proj_w = jax.random.uniform(ks[5], (DI, DR), jnp.float32, -dt_std, dt_std)
        dt = jnp.exp(jax.random.uniform(ks[6], (DI,), jnp.float32) * (math.log(DT_MAX) - math.log(DT_MIN)) + math.log(DT_MIN))
        dt = jnp.clip(dt, DT_FLOOR)
        dt_proj_b = dt + jnp.log(-jnp.expm1(-dt))
        A_log = jnp.log(jnp.broadcast_to(jnp.arange(1, DS + 1, dtype=jnp.float32), (DI, DS)))
        D = jnp.ones((DI,), jnp.float32)
        return dict(hidden_states=hidden_states, z=z, in_proj_w=in_proj_w, conv_w=conv_w, conv_b=conv_b, x_proj_w=x_proj_w, dt_proj_w=dt_proj_w, dt_proj_b=dt_proj_b, A_log=A_log, D=D)
    _L0_xattn_all = _L0_xattn_setup()
    _L0_xattn_in = {k: v for k, v in _L0_xattn_all.items() if k in ('in_proj_w', 'conv_w', 'conv_b', 'x_proj_w', 'dt_proj_w', 'dt_proj_b', 'A_log', 'D')}
    del _L0_xattn_all

    def _L0_ffn_setup():
        import jax, jax.numpy as jnp
        import numpy as np
        NUM_EXPERTS = 8
        EXPERTS_PER_TOK = 2
        key = jax.random.key(seed)
        k1, k2, k3, k4, k5 = jax.random.split(key, 5)
        B, T, D, F, E = (4, 128, 256, 128, NUM_EXPERTS)
        return {'x': jax.random.normal(k1, (B, T, D), dtype=jnp.float32), 'router_w': jax.random.normal(k2, (D, E), dtype=jnp.float32) * 0.02, 'gate_proj': jax.random.normal(k3, (E, D, F), dtype=jnp.float32) * 0.02, 'up_proj': jax.random.normal(k4, (E, D, F), dtype=jnp.float32) * 0.02, 'down_proj': jax.random.normal(k5, (E, F, D), dtype=jnp.float32) * 0.02}
    _L0_ffn_all = _L0_ffn_setup()
    _L0_ffn_in = {k: v for k, v in _L0_ffn_all.items() if k in ('router_w', 'gate_proj', 'up_proj', 'down_proj')}
    del _L0_ffn_all
    return {'x': x, 'ctx_1024': ctx_1024, 'g_xattn': g_xattn, 'g_ffn': g_ffn, 'L0_xattn_in_proj_w': _L0_xattn_in['in_proj_w'], 'L0_xattn_conv_w': _L0_xattn_in['conv_w'], 'L0_xattn_conv_b': _L0_xattn_in['conv_b'], 'L0_xattn_x_proj_w': _L0_xattn_in['x_proj_w'], 'L0_xattn_dt_proj_w': _L0_xattn_in['dt_proj_w'], 'L0_xattn_dt_proj_b': _L0_xattn_in['dt_proj_b'], 'L0_xattn_A_log': _L0_xattn_in['A_log'], 'L0_xattn_D': _L0_xattn_in['D'], 'L0_ffn_router_w': _L0_ffn_in['router_w'], 'L0_ffn_gate_proj': _L0_ffn_in['gate_proj'], 'L0_ffn_up_proj': _L0_ffn_in['up_proj'], 'L0_ffn_down_proj': _L0_ffn_in['down_proj']}

def reference(x, ctx_1024, g_xattn, g_ffn, L0_xattn_in_proj_w, L0_xattn_conv_w, L0_xattn_conv_b, L0_xattn_x_proj_w, L0_xattn_dt_proj_w, L0_xattn_dt_proj_b, L0_xattn_A_log, L0_xattn_D, L0_ffn_router_w, L0_ffn_gate_proj, L0_ffn_up_proj, L0_ffn_down_proj):
    import jax
    import jax.numpy as jnp

    def _L0_xattn_ref(hidden_states, z, in_proj_w, conv_w, conv_b, x_proj_w, dt_proj_w, dt_proj_b, A_log, D):
        import jax, jax.numpy as jnp
        import numpy as np
        import math
        B, L, DM = (2, 256, 128)
        DS, DC, EXP = (16, 4, 2)
        DI = EXP * DM
        DR = math.ceil(DM / 16)
        DT_MIN, DT_MAX, DT_FLOOR = (0.001, 0.1, 0.0001)

        def _ssm_forward(hidden_states, z, in_proj_w, conv_w, conv_b, x_proj_w, dt_proj_w, dt_proj_b, A_log, D):
            b = hidden_states.shape[0]
            x = jnp.einsum('ed,bld->bel', in_proj_w, hidden_states)
            xp = jnp.pad(x, ((0, 0), (0, 0), (DC - 1, 0)))
            xc = jax.lax.conv_general_dilated(xp, conv_w[:, None, :], window_strides=(1,), padding='VALID', dimension_numbers=('NCH', 'OIH', 'NCH'), feature_group_count=DI)
            u = jax.nn.silu(xc + conv_b[None, :, None])
            x_dbl = jnp.einsum('ke,bel->bkl', x_proj_w, u)
            dt_lo = x_dbl[:, :DR]
            Bm = x_dbl[:, DR:DR + DS]
            Cm = x_dbl[:, DR + DS:]
            delta = jax.nn.softplus(jnp.einsum('er,brl->bel', dt_proj_w, dt_lo) + dt_proj_b[None, :, None])
            A = -jnp.exp(A_log)

            def step(state, xs):
                d_t, B_t, C_t, u_t = xs
                dA = jnp.exp(d_t[..., None] * A)
                state = state * dA + (d_t * u_t)[..., None] * B_t[:, None, :]
                y_t = jnp.einsum('ben,bn->be', state, C_t)
                return (state, y_t)
            xs = (jnp.moveaxis(delta, -1, 0), jnp.moveaxis(Bm, -1, 0), jnp.moveaxis(Cm, -1, 0), jnp.moveaxis(u, -1, 0))
            state0 = jnp.zeros((b, DI, DS), delta.dtype)
            _, ys = jax.lax.scan(step, state0, xs)
            y = jnp.moveaxis(ys, 0, -1)
            y = y + D[None, :, None] * u
            y = y * jax.nn.silu(z)
            return jnp.swapaxes(y, 1, 2)
        return _ssm_forward(hidden_states, z, in_proj_w, conv_w, conv_b, x_proj_w, dt_proj_w, dt_proj_b, A_log, D)

    def _L0_ffn_ref(x, router_w, gate_proj, up_proj, down_proj):
        import jax, jax.numpy as jnp
        import numpy as np
        NUM_EXPERTS = 8
        EXPERTS_PER_TOK = 2
        E, K = (NUM_EXPERTS, EXPERTS_PER_TOK)
        scores = jnp.einsum('btd,de->bte', x, router_w).astype(jnp.float32)
        routing_weights, routing_idx = jax.lax.top_k(jax.nn.softmax(scores, axis=-1), K)
        routing_weights = (routing_weights / jnp.sum(routing_weights, axis=-1, keepdims=True)).astype(x.dtype)
        onehot = jax.nn.one_hot(routing_idx, E, dtype=x.dtype)
        dispatch_mask = jnp.sum(onehot, axis=2)
        combine_weights = jnp.einsum('btke,btk->bte', onehot, routing_weights)
        dispatched = x[:, :, None, :] * dispatch_mask[..., None]
        gate = jnp.einsum('bted,edf->btef', dispatched, gate_proj)
        up = jnp.einsum('bted,edf->btef', dispatched, up_proj)
        act = jax.nn.silu(gate) * up
        expert_out = jnp.einsum('btef,efd->bted', act, down_proj)
        return jnp.einsum('bted,bte->btd', expert_out, combine_weights)
    x = x + jnp.tanh(g_xattn[0]) * _L0_xattn_ref(ctx_1024, _layernorm(x, axis=-1), L0_xattn_in_proj_w, L0_xattn_conv_w, L0_xattn_conv_b, L0_xattn_x_proj_w, L0_xattn_dt_proj_w, L0_xattn_dt_proj_b, L0_xattn_A_log, L0_xattn_D)
    x = x + jnp.tanh(g_ffn[0]) * _L0_ffn_ref(_layernorm(x, axis=-1), L0_ffn_router_w, L0_ffn_gate_proj, L0_ffn_up_proj, L0_ffn_down_proj)
    return x

_drawn_inputs = setup_inputs


def setup_inputs(seed=0):
    import zlib

    import numpy as np

    out = dict(_drawn_inputs(seed))
    spreads = {'L0_xattn_conv_b': (0.0, 0.1), 'L0_xattn_D': (1.0, 0.2)}
    factors = {'L0_xattn_dt_proj_w': 7.952,
     'L0_xattn_dt_proj_b': 3.297,
     'L0_xattn_A_log': 2.894,
     'L0_ffn_router_w': 8.0,
     'L0_ffn_gate_proj': 7.416,
     'L0_ffn_up_proj': 7.331,
     'L0_ffn_down_proj': 7.387}
    for name, (base, spread) in spreads.items():
        noise = np.random.default_rng([zlib.crc32(name.encode()), seed]).standard_normal(out[name].shape)
        drawn = base * np.exp(spread * noise) if base else spread * noise
        out[name] = jnp.asarray(drawn.astype(out[name].dtype))
    for name, factor in factors.items():
        out[name] = (out[name] * factor).astype(out[name].dtype)
    return out
```

```python
import concourse.bass as bass
from concourse import mybir
from contextlib import ExitStack



def mamba_moe_program(nc, x, ctx_t, w_in_t, conv_w_t, cols, w_x, w_dt_t, w_router, w_gate, w_up, w_down,
                      gains, consts, out):
    fp32 = mybir.dt.float32
    bf16 = mybir.dt.bfloat16
    u32 = mybir.dt.uint32
    ALU = mybir.AluOpType
    ACT = mybir.ActivationFunctionType

    P = 128
    B, L, DI = x.shape
    EC = DI // P
    TC = L // P
    DM = ctx_t.shape[0]
    TAPS = conv_w_t.shape[0] // DI
    NS = 16
    NE = w_router.shape[2]
    NP = NE // 2
    F = w_down.shape[0]
    DR = w_dt_t.shape[0]
    DT0 = 96
    XW = DT0 + DR
    PAD = TAPS - 1
    EPS = 1e-5
    assert EC == 2 and TC == 2 and DM == P and F == P and EC * L == 512

    T_USES = NS + 2
    M_USES = 4 + NS // 2
    G_USES = 1 + NP
    U_USES = 1 + 2 * NP
    RING = 4
    PCHAIN = 9
    FCHAIN = 12
    FVAR = 5

    ctx = ExitStack()
    with ctx:
        def sb(name, shape, dt=fp32):
            return ctx.enter_context(nc.sbuf_tensor(name, shape, dt))

        def bank(name):
            return ctx.enter_context(nc.psum_tensor(name, [P, 512], fp32))

        def sem(name):
            return ctx.enter_context(nc.semaphore(name))

        x_sb = sb("x_sb", [P, B, TC, DI])
        ctx_sb = sb("ctx_sb", [P, B, PAD + L])
        win_sb = sb("win_sb", [P, DI])
        convw_sb = sb("convw_sb", [P, TAPS, DI])
        wk_sb = sb("wk_sb", [P, TAPS, DI])
        cols_sb = sb("cols_sb", [P, 3 * EC + EC * NS])
        convb = cols_sb[:, 0:EC]
        dtb = cols_sb[:, EC:2 * EC]
        dcol = cols_sb[:, 2 * EC:3 * EC]
        alog = cols_sb[:, 3 * EC:3 * EC + EC * NS]
        a_exp = sb("a_exp", [P, EC * NS])
        a_neg = sb("a_neg", [P, EC, NS])
        wx_sb = sb("wx_sb", [P, EC, XW + NS])
        wdt_sb = sb("wdt_sb", [P, DI])
        router_sb = sb("router_sb", [P, EC, NE])
        gate_sb = sb("gate_sb", [P, NE, EC, F])
        up_sb = sb("up_sb", [P, NE, EC, F])
        down_sb = sb("down_sb", [P, NE, DI])
        gains_sb = sb("gains_sb", [P, 2])
        tg = sb("tg", [P, 2])
        consts_sb = sb("consts_sb", [P, P + 32 + NE + 1])
        ident = consts_sb[:, 0:P]
        pick_f = consts_sb[0:DT0, P:P + 32]
        iota = consts_sb[:, P + 32:P + 32 + NE]
        minus_half = consts_sb[:, P + 32 + NE:P + 32 + NE + 1]
        pick = sb("pick", [DT0, 32], bf16)
        diag_d = sb("diag_d", [P, EC, P])

        zst = sb("zst", [P, B * TC, 6])
        zmv = sb("zmv", [P, B * TC, 2])
        zve = sb("zve", [P, B * TC])
        zrs = sb("zrs", [P, B * TC])
        znm = sb("znm", [P, B * TC])
        sz = sb("sz", [P, TC, L])

        u = sb("u", [P, EC, L])
        xs = sb("xs", [XW, L])
        part3 = sb("part3", [DT0, L], bf16)
        rest1 = sb("rest1", [DT0, L])
        mid64 = sb("mid64", [DT0, L], bf16)
        rest2 = sb("rest2", [DT0, L])
        pre = sb("pre", [P, EC, L])
        nabs = sb("nabs", [P, EC, L])
        texp = sb("texp", [P, EC, L])
        tp1 = sb("tp1", [P, EC, L])
        tln = sb("tln", [P, EC, L])
        nfix = sb("nfix", [P, EC, L])
        sp = sb("sp", [P, EC, L])
        c_next = sb("c_next", [P, TC, NS])
        b_all = sb("b_all", [P, NS, L])

        delta = sb("delta", [P, EC, L])
        du = sb("du", [P, EC, L])
        c_t = sb("c_t", [P, TC, NS])
        dbu = sb("dbu", [P, RING, EC, L])
        h = sb("h", [P, RING, EC, L])
        acc = sb("acc", [P, TC, DI])
        yg = sb("yg", [P, TC, DI])
        x1 = sb("x1", [P, TC, DI])

        fst = sb("fst", [P, TC, 6])
        fmv = sb("fmv", [P, TC, 2])
        fve = sb("fve", [P, TC])
        frs = sb("frs", [P, TC])
        xn = sb("xn", [P, TC, DI])
        xnt = sb("xnt", [P, EC, L])
        sc = sb("sc", [P, TC, NE])
        smax = sb("smax", [P, TC])
        esc = sb("esc", [P, TC, NE])
        top = sb("top", [P, TC, 8])
        topi = sb("topi", [P, TC, 8], u32)
        topf = sb("topf", [P, TC, 8])
        tsum = sb("tsum", [P, TC])
        trec = sb("trec", [P, TC])
        hot1 = sb("hot1", [P, TC, NE])
        hot2 = sb("hot2", [P, TC, NE])
        wt = sb("wt", [P, TC, NE])
        gpre = sb("gpre", [P, NP, 2 * L])
        gs = sb("gs", [P, NP, 2 * L])
        wbc = sb("wbc", [P, NP, 2 * L])
        gw = sb("gw", [P, NP, 2 * L])
        hid = sb("hid", [P, 2, 2 * L])
        out_sb = sb("out_sb", [P, TC, DI])

        da = [bank("da0"), bank("da1")]
        tb = [bank("tb0"), bank("tb1")]
        gb, ub, ob, mb = bank("gb"), bank("ub"), bank("ob"), bank("mb")

        ld_ctx, ld_in, ld_x, ld_col = sem("ld_ctx"), sem("ld_in"), sem("ld_x"), sem("ld_col")
        ld_wx, ld_ffn = sem("ld_wx"), sem("ld_ffn")
        pad_ready, wk_ready, pick_ready = sem("pad_ready"), sem("wk_ready"), sem("pick_ready")
        aexp_ready, a_ready, diag_ready, tanh_ready = sem("aexp_ready"), sem("a_ready"), sem("diag_ready"), sem("tanh_ready")
        zchain, zrs_ready, zn_ready = sem("zchain"), sem("zrs_ready"), sem("zn_ready")
        m_full, m_read = sem("m_full"), sem("m_read")
        high_ready, pchain, texp_ready, tln_ready = sem("high_ready"), sem("pchain"), sem("texp_ready"), sem("tln_ready")
        delta_ready, du_ready, c_ready = sem("delta_ready"), sem("du_ready"), sem("c_ready")
        da_ready, dbu_ready, scan_done = sem("da_ready"), sem("dbu_ready"), sem("scan_done")
        t_full, t_read, sz_ready, x1_ready = sem("t_full"), sem("t_read"), sem("sz_ready"), sem("x1_ready")
        fchain, frs_ready, xn_ready, esc_ready = sem("fchain"), sem("frs_ready"), sem("xn_ready"), sem("esc_ready")
        w_ready, g_full, g_read, u_full, u_read = sem("w_ready"), sem("g_full"), sem("g_read"), sem("u_full"), sem("u_read")
        gs_ready, gw_ready, down_done = sem("gs_ready"), sem("gw_ready"), sem("down_done")
        out_ready, out_stored = sem("out_ready"), sem("out_stored")

        block = ctx.enter_context(nc.Block())

        @block.sync
        def _(sp_):
            sp_.dma_start(win_sb[:, :], w_in_t).then_inc(ld_in, 16)
            sp_.dma_start(convw_sb[:, :, :].rearrange("p k e -> p (k e)"),
                          conv_w_t.partition_broadcast(P)).then_inc(ld_in, 16)
            sp_.dma_start(ctx_sb[:, :, PAD:PAD + L], ctx_t).then_inc(ld_ctx, 16)
            sp_.dma_start(cols_sb[:, :], cols).then_inc(ld_col, 16)
            sp_.dma_start(consts_sb[:, :], consts).then_inc(ld_col, 16)
            sp_.dma_start(gains_sb[:, :], gains.partition_broadcast(P)).then_inc(ld_col, 16)
            sp_.dma_start(wx_sb[:, :, :], w_x).then_inc(ld_wx, 16)
            sp_.dma_start(wdt_sb[DT0:DT0 + DR, :], w_dt_t).then_inc(ld_wx, 16)
            sp_.dma_start(router_sb[:, :, :], w_router).then_inc(ld_ffn, 16)
            sp_.dma_start(gate_sb[:, :, :, :], w_gate).then_inc(ld_ffn, 16)
            sp_.dma_start(up_sb[:, :, :, :], w_up).then_inc(ld_ffn, 16)
            sp_.dma_start(down_sb[:, :, :], w_down).then_inc(ld_ffn, 16)

            def store(b):
                sp_.wait_ge(out_ready, b + 1)
                sp_.dma_start(out[b].rearrange("(c p) e -> p c e", p=P), out_sb[:, :, :]).then_inc(out_stored, 16)

            store(0)
            with sp_.Fori(1, B - 1) as b:
                store(b)
            store(B - 1)
            sp_.wait_ge(out_stored, 16 * B)

        @block.gpsimd
        def _(gp):
            gp.memset(ctx_sb[:, :, 0:PAD], 0.0).then_inc(pad_ready, 1)
            gp.wait_ge(ld_col, 48)
            gp.wait_ge(zchain, 3 * B * TC)
            gp.tensor_tensor(zrs[:, :], zve[:, :], minus_half.to_broadcast([P, B * TC]), ALU.pow)\
              .then_inc(zrs_ready, 1)

            def state_input(b, n, first):
                if n == 0:
                    gp.wait_ge(du_ready, b + 1)
                if n % 2 == 0:
                    gp.wait_ge(m_read, M_USES * b + 4 + n // 2 + 1)
                if not first or n >= RING:
                    gp.wait_ge(scan_done, NS * b + n - RING + 1)
                gp.tensor_tensor(dbu[:, n % RING, :, :], du[:, :, :],
                                 b_all[:, n, :].unsqueeze(1).to_broadcast([P, EC, L]), ALU.mult)\
                  .then_inc(dbu_ready, 1)

            def inv_std(b):
                gp.wait_ge(fchain, FCHAIN * b + FVAR)
                gp.tensor_tensor(frs[:, :], fve[:, :], minus_half.to_broadcast([P, TC]), ALU.pow)\
                  .then_inc(frs_ready, 1)

            def weigh(b, j, first):
                gp.wait_ge(gs_ready, NP * b + j + 1)
                gp.wait_ge(u_read, U_USES * b + 1 + j + 1)
                if not first:
                    gp.wait_ge(u_read, U_USES * (b - 1) + 1 + NP + j + 1)
                gp.tensor_tensor(gw[:, j, :], gs[:, j, :], wbc[:, j, :], ALU.mult).then_inc(gw_ready, 1)

            def body(b, first, ffn, ffn_first):
                for n in range(NS):
                    state_input(b, n, first)
                    if ffn and n == 4:
                        inv_std(b - 1)
                    if ffn and 11 <= n < 11 + NP:
                        weigh(b - 1, n - 11, ffn_first)

            body(0, True, False, False)
            body(1, False, True, True)
            with gp.Fori(2, B) as b:
                body(b, False, True, False)
            inv_std(B - 1)
            for j in range(NP):
                weigh(B - 1, j, False)

        @block.scalar
        def _(act):
            act.dma_start(x_sb[:, :, :, :], x.rearrange("b (c p) e -> p b c e", p=P)).then_inc(ld_x, 16)
            act.wait_ge(ld_col, 48)
            act.activation(a_exp[:, :], alog, ACT.Exp).then_inc(aexp_ready, 1)
            act.activation(tg[:, :], gains_sb[:, :], ACT.Tanh).then_inc(tanh_ready, 1)
            act.activation(pick[:, :], pick_f, ACT.Copy).then_inc(pick_ready, 1)

            def conv_silu(b, first):
                act.wait_ge(m_full, M_USES * b + 1)
                if not first:
                    act.wait_ge(du_ready, b)
                    act.wait_ge(t_full, T_USES * (b - 1) + 1)
                for c in range(EC):
                    last = act.activation(u[:, c, :], mb[:, c * L:(c + 1) * L], ACT.Silu, bias=convb[:, c:c + 1])
                last.then_inc(m_read, 1)

            def x_proj_out(b):
                act.wait_ge(m_full, M_USES * b + 2)
                act.activation(xs[:, :], mb[0:XW, 0:L], ACT.Copy).then_inc(m_read, 1)
                act.wait_ge(m_read, M_USES * b + 2)
                act.activation(part3[:, :], xs[0:DT0, :], ACT.Copy).then_inc(high_ready, 1)

            def dt_out(b):
                act.wait_ge(m_full, M_USES * b + 3)
                for c in range(EC):
                    last = act.activation(pre[:, c, :], mb[:, c * L:(c + 1) * L], ACT.Identity, bias=dtb[:, c:c + 1])
                last.then_inc(m_read, 1)

            def c_out(b, first):
                act.wait_ge(m_full, M_USES * b + 4)
                if not first:
                    act.wait_ge(c_ready, b)
                act.activation(c_next[:, :, :].rearrange("p c n -> p (c n)"), mb[:, 0:TC * NS], ACT.Copy)\
                   .then_inc(m_read, 1)

            def softplus_exp(b):
                act.wait_ge(pchain, PCHAIN * b + 6)
                act.activation(texp[:, :, :], nabs[:, :, :], ACT.Exp).then_inc(texp_ready, 1)

            def softplus_ln(b):
                act.wait_ge(pchain, PCHAIN * b + 7)
                act.activation(tln[:, :, :], tp1[:, :, :], ACT.Ln).then_inc(tln_ready, 1)

            def b_out(b, j, first):
                act.wait_ge(m_full, M_USES * b + 5 + j)
                if not first:
                    act.wait_ge(dbu_ready, NS * (b - 1) + 2 * j + 2)
                act.activation(b_all[:, 2 * j:2 * j + 2, :].rearrange("p n l -> p (n l)"), mb[:, :], ACT.Copy)\
                   .then_inc(m_read, 1)

            def decay(b, n, first):
                if n == 0:
                    act.wait_ge(delta_ready, b + 1)
                if not first or n >= 2:
                    act.wait_ge(scan_done, NS * b + n - 1)
                for c in range(EC):
                    last = act.activation(da[n % 2][:, c * L + 1:(c + 1) * L], delta[:, c, 1:L], ACT.Exp,
                                          scale=a_neg[:, c, n:n + 1])
                last.then_inc(da_ready, 1)

            def skip_term(b, first):
                act.wait_ge(t_full, T_USES * b + 1)
                if not first:
                    act.wait_ge(t_read, T_USES * b)
                act.activation(acc[:, :, :].rearrange("p c e -> p (c e)"), tb[0][:, :], ACT.Copy)\
                   .then_inc(t_read, 1)

            def z_silu(b, first):
                if first:
                    act.wait_ge(zn_ready, 1)
                    act.wait_ge(ld_x, 16)
                else:
                    act.wait_ge(t_full, T_USES * b)
                for c in range(TC):
                    k = TC * b + c
                    last = act.activation(sz[:, c, :], x_of(b)[:, c, :], ACT.Silu,
                                          bias=znm_of(b)[:, c:c + 1], scale=zrs_of(b)[:, c:c + 1])
                last.then_inc(sz_ready, 1)

            def x_of(b):
                return x_sb[:, b, :, :]

            def znm_of(b):
                return znm[:, :].rearrange("p (b c) -> p b c", c=TC)[:, b, :]

            def zrs_of(b):
                return zrs[:, :].rearrange("p (b c) -> p b c", c=TC)[:, b, :]

            def xn_out(b, first):
                act.wait_ge(g_full, G_USES * b + 1)
                if not first:
                    act.wait_ge(u_full, U_USES * b)
                act.activation(xnt[:, :, :].rearrange("p c l -> p (c l)"), gb[:, :], ACT.Copy).then_inc(g_read, 1)

            def router_exp(b):
                act.wait_ge(fchain, FCHAIN * b + FVAR + 1)
                for c in range(TC):
                    last = act.activation(esc[:, c, :], sc[:, c, :], ACT.Exp, bias=smax[:, c:c + 1])
                last.then_inc(esc_ready, 1)

            def weight_out(b, j, first):
                act.wait_ge(u_full, U_USES * b + 2 + j)
                if not first:
                    act.wait_ge(gw_ready, NP * (b - 1) + j + 1)
                act.activation(wbc[:, j, :], ub[:, :], ACT.Copy).then_inc(u_read, 1)

            def gate_out(b, j):
                act.wait_ge(g_full, G_USES * b + 2 + j)
                act.activation(gpre[:, j, :], gb[:, :], ACT.Copy).then_inc(g_read, 1)

            def gate_silu(b, j, first):
                act.wait_ge(g_read, G_USES * b + 2 + j)
                if not first:
                    act.wait_ge(gw_ready, NP * (b - 1) + j + 1)
                act.activation(gs[:, j, :], gpre[:, j, :], ACT.Silu).then_inc(gs_ready, 1)

            def body(b, first, ffn, ffn_first, proj):
                for n in range(NS):
                    decay(b, n, first)
                    if n == 1:
                        skip_term(b, first)
                    if ffn and n == 3:
                        xn_out(b - 1, ffn_first)
                    if ffn and n == 4:
                        router_exp(b - 1)
                    if ffn and 4 <= n < 4 + NP:
                        gate_out(b - 1, n - 4)
                    if ffn and 7 <= n < 7 + NP:
                        weight_out(b - 1, n - 7, ffn_first)
                    if n == 7:
                        z_silu(b, first)
                        if proj:
                            conv_silu(b + 1, False)
                        if ffn:
                            for j in range(NP):
                                gate_silu(b - 1, j, ffn_first)
                    if proj and n == 9:
                        x_proj_out(b + 1)
                    if proj and n == 10:
                        dt_out(b + 1)
                        c_out(b + 1, False)
                    if proj and n == 11:
                        softplus_exp(b + 1)
                    if proj and n == 12:
                        softplus_ln(b + 1)
                        b_out(b + 1, 0, False)
                    if proj and n == 13:
                        b_out(b + 1, 1, False)
                        b_out(b + 1, 2, False)
                    if proj and n == 14:
                        b_out(b + 1, 3, False)
                        b_out(b + 1, 4, False)
                    if proj and n == 15:
                        b_out(b + 1, 5, False)
                        b_out(b + 1, 6, False)
                        b_out(b + 1, 7, False)

            conv_silu(0, True)
            x_proj_out(0)
            dt_out(0)
            c_out(0, True)
            softplus_exp(0)
            softplus_ln(0)
            for j in range(NS // 2):
                b_out(0, j, True)
            act.wait_ge(a_ready, 1)
            body(0, True, False, False, True)
            body(1, False, True, True, True)
            with act.Fori(2, B - 1) as b:
                body(b, False, True, False, True)
            body(B - 1, False, True, False, False)
            xn_out(B - 1, False)
            router_exp(B - 1)
            for j in range(NP):
                gate_out(B - 1, j)
                gate_silu(B - 1, j, False)
            for j in range(NP):
                weight_out(B - 1, j, False)

        @block.vector
        def _(dve):
            for n in range(2):
                dve.memset(da[n][:, :], 0.0).then_inc(a_ready, 1)

            dve.wait_ge(ld_in, 32)
            dve.tensor_tensor(wk_sb[:, :, :], convw_sb[:, :, :],
                              win_sb[:, :].unsqueeze(1).to_broadcast([P, TAPS, DI]), ALU.mult).then_inc(wk_ready, 1)
            dve.wait_ge(ld_x, 16)
            for k in range(B * TC):
                dve.bn_stats(zst[:, k, :], x_sb[:, k // TC, k % TC, :]).then_inc(zchain, 1)
            for k in range(B * TC):
                dve.wait_ge(zchain, B * TC)
                dve.bn_aggr(zmv[:, k, :], zst[:, k, :]).then_inc(zchain, 1)
            for k in range(B * TC):
                dve.wait_ge(zchain, 2 * B * TC)
                dve.tensor_scalar(zve[:, k:k + 1], zmv[:, k, 1:2], EPS, None, ALU.add).then_inc(zchain, 1)
            dve.wait_ge(ld_col, 48)
            for c in range(EC):
                last = dve.tensor_scalar(diag_d[:, c, :], ident, dcol[:, c:c + 1], None, ALU.mult)
            last.then_inc(diag_ready, 1)
            dve.wait_ge(aexp_ready, 1)
            dve.tensor_scalar(a_neg[:, :, :].rearrange("p c n -> p (c n)"), a_exp[:, :], -1.0, None, ALU.mult)\
               .then_inc(a_ready, 1)

            def z_shift():
                dve.wait_ge(zrs_ready, 1)
                dve.scalar_tensor_tensor(znm[:, :], zmv[:, :, 0], -1.0, zrs[:, :], ALU.mult, ALU.mult)\
                   .then_inc(zn_ready, 1)

            def split_b(b):
                k = PCHAIN * b
                dve.wait_ge(high_ready, b + 1)
                dve.tensor_tensor(rest1[:, :], xs[0:DT0, :], part3[:, :], ALU.subtract).then_inc(pchain, 1)
                dve.wait_ge(pchain, k + 1)
                dve.tensor_copy(mid64[:, :], rest1[:, :]).then_inc(pchain, 1)
                dve.wait_ge(pchain, k + 2)
                dve.tensor_tensor(rest2[:, :], rest1[:, :], mid64[:, :], ALU.subtract).then_inc(pchain, 1)
                dve.tensor_copy(part3[32:64, :], mid64[32:64, :]).then_inc(pchain, 1)
                dve.wait_ge(pchain, k + 3)
                dve.tensor_copy(part3[64:96, :], rest2[64:96, :]).then_inc(pchain, 1)

            def softplus_abs(b):
                dve.wait_ge(m_read, M_USES * b + 3)
                dve.scalar_tensor_tensor(flat(nabs), flat(pre), -1.0, flat(pre), ALU.mult, ALU.min)\
                   .then_inc(pchain, 1)

            def softplus_one(b):
                dve.wait_ge(texp_ready, b + 1)
                dve.tensor_scalar(flat(tp1), flat(texp), 1.0, None, ALU.add).then_inc(pchain, 1)

            def softplus_fix(b):
                dve.wait_ge(pchain, PCHAIN * b + 7)
                dve.scalar_tensor_tensor(flat(nfix), flat(tp1), -1.0, flat(texp), ALU.add, ALU.subtract)\
                   .then_inc(pchain, 1)

            def softplus_sum(b):
                dve.wait_ge(tln_ready, b + 1)
                dve.scalar_tensor_tensor(flat(sp), flat(pre), 0.0, flat(tln), ALU.max, ALU.add).then_inc(pchain, 1)

            def flat(t):
                return t[:, :, :].rearrange("p c l -> p (c l)")

            def take_projections(b, first):
                dve.wait_ge(pchain, PCHAIN * b + 9)
                if not first:
                    dve.wait_ge(da_ready, NS * b)
                dve.tensor_tensor(flat(delta), flat(sp), flat(nfix), ALU.subtract).then_inc(delta_ready, 1)
                dve.wait_ge(delta_ready, b + 1)
                dve.wait_ge(m_read, M_USES * b + 1)
                if not first:
                    dve.wait_ge(dbu_ready, NS * b)
                dve.tensor_tensor(flat(du), flat(delta), flat(u), ALU.mult).then_inc(du_ready, 1)

            def take_c(b):
                dve.wait_ge(m_read, M_USES * b + 4)
                dve.tensor_copy(c_t[:, :, :], c_next[:, :, :]).then_inc(c_ready, 1)

            def scan(b, n, first):
                dve.wait_ge(da_ready, NS * b + n + 1)
                dve.wait_ge(dbu_ready, NS * b + n + 1)
                if n >= RING:
                    dve.wait_ge(t_full, T_USES * b + n - RING + 2)
                elif not first:
                    dve.wait_ge(t_full, T_USES * (b - 1) + NS + n - RING + 2)
                dve.tensor_tensor_scan(h[:, n % RING, :, :].rearrange("p c l -> p (c l)"), da[n % 2][:, :],
                                       dbu[:, n % RING, :, :].rearrange("p c l -> p (c l)"), 0.0,
                                       ALU.mult, ALU.add).then_inc(scan_done, 1)

            def add_state(b, n):
                dve.wait_ge(t_full, T_USES * b + n + 2)
                dve.wait_ge(t_read, T_USES * b + n + 1)
                if n == 0:
                    dve.wait_ge(c_ready, b + 1)
                src = tb[(n + 1) % 2]
                for c in range(TC):
                    last = dve.scalar_tensor_tensor(acc[:, c, :], src[:, c * DI:(c + 1) * DI], c_t[:, c, n:n + 1],
                                                    acc[:, c, :], ALU.mult, ALU.add)
                last.then_inc(t_read, 1)

            def gate_y(b, first):
                dve.wait_ge(t_full, T_USES * (b + 1))
                dve.wait_ge(t_read, T_USES * (b + 1) - 1)
                dve.tensor_tensor(flat(yg), tb[(NS + 1) % 2][:, :], flat(acc), ALU.mult).then_inc(t_read, 1)
                dve.wait_ge(t_read, T_USES * (b + 1))
                if first:
                    dve.wait_ge(tanh_ready, 1)
                dve.scalar_tensor_tensor(flat(x1), flat(yg), tg[:, 0:1],
                                         x_sb[:, b, :, :].rearrange("p c e -> p (c e)"), ALU.mult, ALU.add)\
                   .then_inc(x1_ready, 1)

            def row_stats(b):
                k = FCHAIN * b
                dve.wait_ge(x1_ready, b + 1)
                for c in range(TC):
                    dve.bn_stats(fst[:, c, :], x1[:, c, :]).then_inc(fchain, 1)
                dve.wait_ge(fchain, k + TC)
                for c in range(TC):
                    dve.bn_aggr(fmv[:, c, :], fst[:, c, :]).then_inc(fchain, 1)
                dve.wait_ge(fchain, k + 2 * TC)
                dve.tensor_scalar(fve[:, :], fmv[:, :, 1], EPS, None, ALU.add).then_inc(fchain, 1)

            def normalise(b):
                dve.wait_ge(frs_ready, b + 1)
                for c in range(TC):
                    last = dve.tensor_scalar(xn[:, c, :], x1[:, c, :], fmv[:, c, 0:1], frs[:, c:c + 1],
                                             ALU.subtract, ALU.mult)
                last.then_inc(xn_ready, 1)

            def router_max(b):
                dve.wait_ge(u_full, U_USES * b + 1)
                dve.tensor_copy(sc[:, :, :].rearrange("p c e -> p (c e)"), ub[:, 0:TC * NE]).then_inc(u_read, 1)
                dve.wait_ge(u_read, U_USES * b + 1)
                dve.tensor_reduce(smax[:, :], sc[:, :, :], mybir.AxisListType.X, ALU.max, negate=True)\
                   .then_inc(fchain, 1)

            def router_weights(b):
                k = FCHAIN * b + FVAR + 1
                dve.wait_ge(esc_ready, b + 1)
                for c in range(TC):
                    dve.max(top[:, c, :], esc[:, c, :]).then_inc(fchain, 1)
                dve.wait_ge(fchain, k + TC)
                for c in range(TC):
                    dve.max_index(topi[:, c, :], top[:, c, :], esc[:, c, :])
                last = dve.tensor_tensor(tsum[:, :], top[:, :, 0], top[:, :, 1], ALU.add)
                last.then_inc(fchain, 1)
                dve.wait_ge(fchain, k + TC + 1)
                dve.tensor_copy(topf[:, :, 0:2], topi[:, :, 0:2]).then_inc(fchain, 1)
                dve.reciprocal(trec[:, :], tsum[:, :])
                dve.wait_ge(fchain, k + TC + 2)
                for c in range(TC):
                    last = dve.tensor_scalar(hot1[:, c, :], iota, topf[:, c, 0:1], None, ALU.is_equal)
                last.then_inc(fchain, 1)
                dve.wait_ge(fchain, k + TC + 3)
                for c in range(TC):
                    last = dve.scalar_tensor_tensor(hot2[:, c, :], iota, topf[:, c, 1:2], hot1[:, c, :],
                                                    ALU.is_equal, ALU.add)
                last.then_inc(fchain, 1)
                dve.wait_ge(fchain, k + TC + 4)
                for c in range(TC):
                    last = dve.scalar_tensor_tensor(wt[:, c, :], esc[:, c, :], trec[:, c:c + 1], hot2[:, c, :],
                                                    ALU.mult, ALU.mult)
                last.then_inc(w_ready, 1)

            def hidden(b, j, first):
                dve.wait_ge(gw_ready, NP * b + j + 1)
                dve.wait_ge(u_full, U_USES * b + 2 + NP + j)
                if j >= 2:
                    dve.wait_ge(down_done, NP * b + j - 1)
                elif not first:
                    dve.wait_ge(down_done, NP * (b - 1) + NP - 1 + j)
                dve.tensor_tensor(hid[:, j % 2, :], ub[:, :], gw[:, j, :], ALU.mult).then_inc(u_read, 1)

            def finish(b, first):
                dve.wait_ge(down_done, NP * (b + 1))
                if not first:
                    dve.wait_ge(out_stored, 16 * b)
                dve.scalar_tensor_tensor(flat(out_sb), ob[:, :], tg[:, 1:2], flat(x1), ALU.mult, ALU.add)\
                   .then_inc(out_ready, 1)

            def body(b, first, ffn, ffn_first, proj):
                for n in range(NS):
                    scan(b, n, first)
                    if n == 0:
                        if not first:
                            add_state(b - 1, NS - 1)
                            gate_y(b - 1, ffn_first)
                            row_stats(b - 1)
                        take_c(b)
                    else:
                        add_state(b, n - 1)
                    if ffn and n == 1:
                        normalise(b - 1)
                    if ffn and n == 3:
                        router_max(b - 1)
                    if ffn and n == 4:
                        router_weights(b - 1)
                    if ffn and 10 <= n < 10 + NP:
                        hidden(b - 1, n - 10, ffn_first)
                    if ffn and n == 15:
                        finish(b - 1, ffn_first)
                    if proj and n == 8:
                        split_b(b + 1)
                    if proj and n == 9:
                        softplus_abs(b + 1)
                    if proj and n == 10:
                        softplus_one(b + 1)
                        softplus_fix(b + 1)
                    if proj and n == 12:
                        softplus_sum(b + 1)
                if proj:
                    take_projections(b + 1, False)

            split_b(0)
            softplus_abs(0)
            softplus_one(0)
            softplus_fix(0)
            softplus_sum(0)
            take_projections(0, True)
            z_shift()
            body(0, True, False, False, True)
            body(1, False, True, True, True)
            with dve.Fori(2, B - 1) as b:
                body(b, False, True, False, True)
            body(B - 1, False, True, False, False)
            last_b = B - 1
            add_state(last_b, NS - 1)
            gate_y(last_b, False)
            row_stats(last_b)
            normalise(last_b)
            router_max(last_b)
            router_weights(last_b)
            for j in range(NP):
                hidden(last_b, j, False)
            finish(last_b, False)

        @block.tensor
        def _(pe):
            def in_proj(b, first):
                if first:
                    pe.wait_ge(ld_ctx, 16)
                    pe.wait_ge(pad_ready, 1)
                    pe.wait_ge(wk_ready, 1)
                else:
                    pe.wait_ge(m_read, M_USES * b)
                for c in range(EC):
                    for k in range(TAPS):
                        last = pe.matmul(mb[:, c * L:(c + 1) * L], wk_sb[:, k, c * P:(c + 1) * P],
                                         ctx_sb[:, b, k:k + L], start=(k == 0), stop=(k == TAPS - 1))
                last.then_inc(m_full, 1)

            def x_proj(b, first):
                if first:
                    pe.wait_ge(ld_wx, 32)
                pe.wait_ge(m_read, M_USES * b + 1)
                for c in range(EC):
                    last = pe.matmul(mb[0:XW, 0:L], wx_sb[:, c, 0:XW], u[:, c, :], start=(c == 0), stop=(c == EC - 1))
                last.then_inc(m_full, 1)

            def dt_proj(b):
                pe.wait_ge(m_read, M_USES * b + 2)
                for c in range(EC):
                    last = pe.matmul(mb[:, c * L:(c + 1) * L], wdt_sb[DT0:XW, c * P:(c + 1) * P], xs[DT0:XW, :],
                                     start=True, stop=True)
                last.then_inc(m_full, 1)

            def c_proj(b):
                pe.wait_ge(m_read, M_USES * b + 3)
                for t in range(TC):
                    for c in range(EC):
                        last = pe.matmul(mb[:, t * NS:(t + 1) * NS], u[:, c, t * P:(t + 1) * P],
                                         wx_sb[:, c, XW:XW + NS], start=(c == 0), stop=(c == EC - 1))
                last.then_inc(m_full, 1)

            def b_spread(b, j, first):
                if j == 0:
                    pe.wait_ge(pchain, PCHAIN * b + 5)
                    if first:
                        pe.wait_ge(pick_ready, 1)
                pe.wait_ge(m_read, M_USES * b + 4 + j)
                for k in range(2):
                    n = 2 * j + k
                    last = pe.matmul(mb[:, k * L:(k + 1) * L], pick[:, n:n + 1].to_broadcast([DT0, P]), part3[:, :],
                                     start=True, stop=True)
                last.then_inc(m_full, 1)

            def skip_term(b, first):
                if first:
                    pe.wait_ge(ld_col, 48)
                    pe.wait_ge(diag_ready, 1)
                else:
                    pe.wait_ge(t_read, T_USES * b - 1)
                pe.wait_ge(m_read, M_USES * b + 1)
                for t in range(TC):
                    for c in range(EC):
                        o = t * DI + c * P
                        last = pe.matmul(tb[0][:, o:o + P], u[:, c, t * P:(t + 1) * P], diag_d[:, c, :],
                                         start=True, stop=True)
                last.then_inc(t_full, 1)

            def turn_state(b, n, first):
                pe.wait_ge(scan_done, NS * b + n + 1)
                if n >= 1:
                    pe.wait_ge(t_read, T_USES * b + n)
                elif not first:
                    pe.wait_ge(t_read, T_USES * b)
                for t in range(TC):
                    for c in range(EC):
                        o = t * DI + c * P
                        last = pe.transpose(tb[(n + 1) % 2][:, o:o + P], h[:, n % RING, c, t * P:(t + 1) * P], ident)
                last.then_inc(t_full, 1)

            def turn_z(b):
                pe.wait_ge(sz_ready, b + 1)
                pe.wait_ge(t_read, T_USES * b + NS)
                for t in range(TC):
                    for c in range(EC):
                        o = t * DI + c * P
                        last = pe.transpose(tb[(NS + 1) % 2][:, o:o + P], sz[:, c, t * P:(t + 1) * P], ident)
                last.then_inc(t_full, 1)

            def turn_xn(b, first):
                pe.wait_ge(xn_ready, b + 1)
                if not first:
                    pe.wait_ge(g_read, G_USES * b)
                for c in range(EC):
                    for t in range(TC):
                        last = pe.transpose(gb[:, c * L + t * P:c * L + (t + 1) * P], xn[:, t, c * P:(c + 1) * P], ident)
                last.then_inc(g_full, 1)

            def router(b, first):
                pe.wait_ge(g_read, G_USES * b + 1)
                if first:
                    pe.wait_ge(ld_ffn, 64)
                else:
                    pe.wait_ge(u_read, U_USES * b)
                for t in range(TC):
                    for c in range(EC):
                        last = pe.matmul(ub[:, t * NE:(t + 1) * NE], xnt[:, c, t * P:(t + 1) * P], router_sb[:, c, :],
                                         start=(c == 0), stop=(c == EC - 1))
                last.then_inc(u_full, 1)

            def spread_weights(b, j):
                if j == 0:
                    pe.wait_ge(w_ready, b + 1)
                pe.wait_ge(u_read, U_USES * b + 1 + j)
                for k in range(2):
                    for t in range(TC):
                        e = 2 * j + k
                        last = pe.matmul(ub[:, k * L + t * P:k * L + (t + 1) * P],
                                         wt[:, t, e:e + 1].to_broadcast([P, P]), ident, start=True, stop=True)
                last.then_inc(u_full, 1)

            def gates(b, j):
                pe.wait_ge(g_read, G_USES * b + 1 + j)
                for k in range(2):
                    for c in range(EC):
                        last = pe.matmul(gb[:, k * L:(k + 1) * L], gate_sb[:, 2 * j + k, c, :], xnt[:, c, :],
                                         start=(c == 0), stop=(c == EC - 1))
                last.then_inc(g_full, 1)

            def ups(b, j):
                pe.wait_ge(u_read, U_USES * b + 1 + NP + j)
                for k in range(2):
                    for c in range(EC):
                        last = pe.matmul(ub[:, k * L:(k + 1) * L], up_sb[:, 2 * j + k, c, :], xnt[:, c, :],
                                         start=(c == 0), stop=(c == EC - 1))
                last.then_inc(u_full, 1)

            def downs(b, j, first):
                pe.wait_ge(u_read, U_USES * b + 2 + NP + j)
                if j == 0 and not first:
                    pe.wait_ge(out_ready, b)
                for k in range(2):
                    for t in range(TC):
                        e = 2 * j + k
                        last = pe.matmul(ob[:, t * DI:(t + 1) * DI], hid[:, j % 2, k * L + t * P:k * L + (t + 1) * P],
                                         down_sb[:, e, :], start=(e == 0 and t == 0), stop=(e == NE - 1),
                                         skip_group_check=True)
                last.then_inc(down_done, 1)

            def body(b, first, ffn, ffn_first, proj):
                if not first:
                    turn_z(b - 1)
                skip_term(b, first)
                for n in range(NS):
                    turn_state(b, n, first)
                    if proj and n == 0:
                        in_proj(b + 1, False)
                    if ffn and n == 1:
                        turn_xn(b - 1, ffn_first)
                    if ffn and n == 2:
                        router(b - 1, ffn_first)
                    if ffn and 2 <= n < 2 + NP:
                        gates(b - 1, n - 2)
                    if ffn and 5 <= n < 5 + NP:
                        spread_weights(b - 1, n - 5)
                    if ffn and 9 <= n < 9 + NP:
                        ups(b - 1, n - 9)
                    if ffn and 11 <= n < 11 + NP:
                        downs(b - 1, n - 11, ffn_first)
                    if proj and n == 7:
                        x_proj(b + 1, False)
                    if proj and n == 8:
                        dt_proj(b + 1)
                    if proj and n == 9:
                        c_proj(b + 1)
                    if proj and n == 10:
                        b_spread(b + 1, 0, False)
                    if proj and n == 11:
                        b_spread(b + 1, 1, False)
                        b_spread(b + 1, 2, False)
                    if proj and n == 12:
                        b_spread(b + 1, 3, False)
                        b_spread(b + 1, 4, False)
                    if proj and n == 13:
                        b_spread(b + 1, 5, False)
                        b_spread(b + 1, 6, False)
                    if proj and n == 14:
                        b_spread(b + 1, 7, False)

            in_proj(0, True)
            x_proj(0, True)
            dt_proj(0)
            c_proj(0)
            for j in range(NS // 2):
                b_spread(0, j, True)
            body(0, True, False, False, True)
            body(1, False, True, True, True)
            with pe.Fori(2, B - 1) as b:
                body(b, False, True, False, True)
            body(B - 1, False, True, False, False)
            last_b = B - 1
            turn_z(last_b)
            turn_xn(last_b, False)
            router(last_b, False)
            for j in range(NP):
                gates(last_b, j)
            for j in range(NP):
                spread_weights(last_b, j)
            for j in range(NP):
                ups(last_b, j)
                if j >= 1:
                    downs(last_b, j - 1, False)
            downs(last_b, NP - 1, False)


def kernel(x, ctx_1024, g_xattn, g_ffn, L0_xattn_in_proj_w, L0_xattn_conv_w, L0_xattn_conv_b, L0_xattn_x_proj_w,
           L0_xattn_dt_proj_w, L0_xattn_dt_proj_b, L0_xattn_A_log, L0_xattn_D, L0_ffn_router_w, L0_ffn_gate_proj,
           L0_ffn_up_proj, L0_ffn_down_proj):
    import numpy as np
    import concourse.bacc as bacc
    from concourse.bass_utils import run_bass_kernel_spmd

    P = 128

    def arr(a):
        return np.asarray(a)

    def by_partition(a):
        a = arr(a)
        return np.swapaxes(a.reshape((a.shape[0] // P, P) + a.shape[1:]), 0, 1)

    xw = arr(L0_xattn_x_proj_w)
    ns = arr(L0_xattn_A_log).shape[1]
    dr = arr(L0_xattn_dt_proj_w).shape[1]
    dt_rows, b_rows, c_rows = xw[:dr], xw[dr:dr + ns], xw[dr + ns:]
    gap = np.zeros((32 - ns, xw.shape[1]), xw.dtype)
    w_x = np.concatenate([b_rows, gap, b_rows, gap, b_rows, gap, dt_rows, c_rows], 0).T
    ne = arr(L0_ffn_router_w).shape[1]
    consts = np.zeros((P, P + 32 + ne + 1), np.float32)
    consts[:, :P] = np.eye(P)
    consts[:, P:P + 32] = np.tile(np.eye(32), (P // 32, 1))
    consts[:, P + 32:P + 32 + ne] = np.arange(ne)
    consts[:, P + 32 + ne] = -0.5
    data = {
        "x": arr(x),
        "ctx_t": np.transpose(arr(ctx_1024), (2, 0, 1)),
        "w_in_t": arr(L0_xattn_in_proj_w).T,
        "conv_w_t": arr(L0_xattn_conv_w).T.reshape(-1),
        "cols": np.concatenate([by_partition(L0_xattn_conv_b), by_partition(L0_xattn_dt_proj_b),
                                by_partition(L0_xattn_D), by_partition(L0_xattn_A_log).reshape(P, -1)], 1),
        "w_x": by_partition(w_x),
        "w_dt_t": arr(L0_xattn_dt_proj_w).T,
        "w_router": by_partition(L0_ffn_router_w),
        "w_gate": np.transpose(arr(L0_ffn_gate_proj).reshape(ne, -1, P, P), (2, 0, 1, 3)),
        "w_up": np.transpose(arr(L0_ffn_up_proj).reshape(ne, -1, P, P), (2, 0, 1, 3)),
        "w_down": np.transpose(arr(L0_ffn_down_proj), (1, 0, 2)),
        "gains": np.concatenate([arr(g_xattn), arr(g_ffn)]),
        "consts": consts,
    }
    nc = bacc.Bacc("TRN2", target_bir_lowering=False, num_devices=1)
    arrays, args = {}, {}
    for name, a in data.items():
        a = np.ascontiguousarray(a)
        arrays[f"in_{name}"] = a
        args[name] = nc.dram_tensor(f"in_{name}", a.shape, mybir.dt.from_np(a.dtype), kind="ExternalInput").ap()
    out = nc.dram_tensor("out", data["x"].shape, mybir.dt.float32, kind="ExternalOutput").ap()
    mamba_moe_program(nc, out=out, **args)
    r = run_bass_kernel_spmd(nc, [arrays], core_ids=[0])
    return r.results[0]["out"]
```

```python
import concourse.bass as bass
from concourse import mybir
from contextlib import ExitStack



def mamba_moe_program(nc, x, ctx_t, w_in_t, conv_w_t, cols, w_x, w_dt_t, w_router, w_gate_up, w_down,
                      gains, consts, out):
    fp32 = mybir.dt.float32
    bf16 = mybir.dt.bfloat16
    fp32r = mybir.dt.float32r
    u32 = mybir.dt.uint32
    ALU = mybir.AluOpType
    ACT = mybir.ActivationFunctionType

    P = 128
    B, L, DI = x.shape
    EC = DI // P
    TC = L // P
    DM = ctx_t.shape[0]
    TAPS = conv_w_t.shape[0] // DI
    NS = 16
    NE = w_router.shape[2]
    F = w_down.shape[0]
    DR = w_dt_t.shape[0]
    DT0 = 96
    C0 = DT0 + DR
    XW = C0 + NS
    PAD = TAPS - 1
    EPS = 1e-5
    assert EC == 2 and TC == 2 and DM == P and F == P and EC * L == 512

    T_USES = NS + 2
    PB = 2
    P_USES = (4 + NS // 2) // PB
    FB = 3
    F_ORDER = ["scores", "gate0", "gate1", "gate2", "up0", "up1", "up2", "turn0", "up3", "turn1", "turn2", "turn3"]
    F_USES = len(F_ORDER) // FB
    O_USES = 3
    O_READS = 1
    RING = 4
    DA = 8
    LEAD = 2
    AHEAD = 2
    QE = 512 // F
    HALVES = NE // QE
    NQ = TC * HALVES

    PCHAIN = 9
    FCHAIN = 12
    FVAR = 5

    ctx = ExitStack()
    with ctx:
        def sb(name, shape, dt=fp32):
            return ctx.enter_context(nc.sbuf_tensor(name, shape, dt))

        def bank(name):
            return ctx.enter_context(nc.psum_tensor(name, [P, 512], fp32))

        def sem(name):
            return ctx.enter_context(nc.semaphore(name))

        x_sb = sb("x_sb", [P, B, TC, DI])
        ctx_sb = sb("ctx_sb", [P, B, PAD + L])
        win_sb = sb("win_sb", [P, DI])
        convw_sb = sb("convw_sb", [P, TAPS, DI])
        wk_sb = sb("wk_sb", [P, TAPS, DI])
        cols_sb = sb("cols_sb", [P, 3 * EC + EC * NS])
        convb = cols_sb[:, 0:EC]
        dtb = cols_sb[:, EC:2 * EC]
        dcol = cols_sb[:, 2 * EC:3 * EC]
        alog = cols_sb[:, 3 * EC:3 * EC + EC * NS]
        a_exp = sb("a_exp", [P, EC * NS])
        a_neg = sb("a_neg", [P, EC, NS])
        wx_sb = sb("wx_sb", [P, EC, XW])
        wdt_sb = sb("wdt_sb", [P, DI])
        router_sb = sb("router_sb", [P, EC, NE])
        raw = sb("raw", [P, EC, 2, NE, F])
        rhi = sb("rhi", [P, EC, NE], fp32r)
        rlo = sb("rlo", [P, EC, NE], fp32r)
        whi = sb("whi", [P, EC, 2, NE, F], fp32r)
        wlo = sb("wlo", [P, EC, 2, NE, F], fp32r)
        down_sb = sb("down_sb", [P, NE, DI])
        gains_sb = sb("gains_sb", [P, 2])
        tg = sb("tg", [P, 2])
        consts_sb = sb("consts_sb", [P, P + 32 + NE + 1])
        ident = consts_sb[:, 0:P]
        pick_f = consts_sb[0:DT0, P:P + 32]
        iota = consts_sb[:, P + 32:P + 32 + NE]
        minus_half = consts_sb[:, P + 32 + NE:P + 32 + NE + 1]
        pick = sb("pick", [DT0, 32], bf16)

        zst = sb("zst", [P, B * TC, 6])
        zmv = sb("zmv", [P, B * TC, 2])
        zve = sb("zve", [P, B * TC])
        zrs = sb("zrs", [P, B, TC])
        znm = sb("znm", [P, B, TC])
        sz = sb("sz", [P, TC, L])

        u = sb("u", [P, EC, L])
        ud = sb("ud", [P, EC, L])
        xs = sb("xs", [XW, L])
        part3 = sb("part3", [DT0, L], bf16)
        rest1 = sb("rest1", [DT0, L])
        mid64 = sb("mid64", [DT0, L], bf16)
        rest2 = sb("rest2", [DT0, L])
        pre = sb("pre", [P, EC, L])
        nabs = sb("nabs", [P, EC, L])
        texp = sb("texp", [P, EC, L])
        tp1 = sb("tp1", [P, EC, L])
        tln = sb("tln", [P, EC, L])
        nfix = sb("nfix", [P, EC, L])
        sp = sb("sp", [P, EC, L])
        c_next = sb("c_next", [P, TC, NS])
        b_all = sb("b_all", [P, NS, L])

        delta = sb("delta", [P, EC, L])
        du = sb("du", [P, EC, L])
        c_t = sb("c_t", [P, TC, NS])
        da = sb("da", [P, DA, EC, L])
        dbu = sb("dbu", [P, RING, EC, L])
        h = sb("h", [P, RING, EC, L])
        acc = sb("acc", [P, TC, DI])
        yg = sb("yg", [P, TC, DI])
        x1 = sb("x1", [P, TC, DI])

        fst = sb("fst", [P, TC, 6])
        fmv = sb("fmv", [P, TC, 2])
        fve = sb("fve", [P, TC])
        frs = sb("frs", [P, TC])
        xn = sb("xn", [P, TC, DI])
        xhi = sb("xhi", [P, EC, L], fp32r)
        xlo = sb("xlo", [P, EC, L], fp32r)
        sc = sb("sc", [P, TC, NE])
        smax = sb("smax", [P, TC])
        esc = sb("esc", [P, TC, NE])
        top = sb("top", [P, TC, 8])
        topi = sb("topi", [P, TC, 8], u32)
        topf = sb("topf", [P, TC, 8])
        tsum = sb("tsum", [P, TC])
        trec = sb("trec", [P, TC])
        hot1 = sb("hot1", [P, TC, NE])
        hot2 = sb("hot2", [P, TC, NE])
        wt = sb("wt", [P, TC, NE])
        gs = sb("gs", [P, NQ, QE * F])
        hid = sb("hid", [P, NQ, QE * F])
        hid_t = sb("hid_t", [P, NQ, QE * P])

        tb = [bank("tb0"), bank("tb1")]
        pb = [bank(f"pb{k}") for k in range(PB)]
        fb = [bank(f"fb{k}") for k in range(FB)]
        ob = bank("ob")

        ld_ctx0, ld_ctx, ld_in, ld_x, ld_col = sem("ld_ctx0"), sem("ld_ctx"), sem("ld_in"), sem("ld_x"), sem("ld_col")
        ld_wx, ld_ffn, ld_down = sem("ld_wx"), sem("ld_ffn"), sem("ld_down")
        pad_ready, wk_ready, pick_ready = sem("pad_ready"), sem("wk_ready"), sem("pick_ready")
        aexp_ready, a_ready, tanh_ready = sem("aexp_ready"), sem("a_ready"), sem("tanh_ready")
        whi_ready, wlo_ready = sem("whi_ready"), sem("wlo_ready")
        zchain, zrs_ready, zn_ready = sem("zchain"), sem("zrs_ready"), sem("zn_ready")
        p_full = [sem(f"p_full{k}") for k in range(PB)]
        p_read = [sem(f"p_read{k}") for k in range(PB)]
        high_ready, pchain, texp_ready, tln_ready = sem("high_ready"), sem("pchain"), sem("texp_ready"), sem("tln_ready")
        delta_ready, du_ready, c_ready = sem("delta_ready"), sem("du_ready"), sem("c_ready")
        da_ready, dbu_ready, scan_done = sem("da_ready"), sem("dbu_ready"), sem("scan_done")
        t_full, t_read, sz_ready, x1_ready = sem("t_full"), sem("t_read"), sem("sz_ready"), sem("x1_ready")
        fchain, frs_ready, xn_ready, esc_ready = sem("fchain"), sem("frs_ready"), sem("xn_ready"), sem("esc_ready")
        xhi_ready, ud_ready, w_ready = sem("xhi_ready"), sem("ud_ready"), sem("w_ready")
        f_full = [sem(f"f_full{k}") for k in range(FB)]
        sc_read = sem("sc_read")
        o_full, o_read = sem("o_full"), sem("o_read")
        gs_ready, gw_ready, hid_ready, hidt_ready = sem("gs_ready"), sem("gw_ready"), sem("hid_ready"), sem("hidt_ready")
        tail_up, tail_turn = sem("tail_up"), sem("tail_turn")
        out_ready, out_stored = sem("out_ready"), sem("out_stored")

        tail_ups = [pb[0], pb[1], tb[0], tb[1]]
        tail_turns = [fb[1], fb[2], fb[0], pb[0]]
        EXP_LN = "natural_log_exp_and_others"

        IN, XP, DT, CP, BP = 0, 1, 2, 3, 4

        PIECES = EC * 2 * HALVES

        def piece(t, k):
            c, what, half = k // (2 * HALVES), k // HALVES % 2, k % HALVES
            return t[:, c, what, half * QE:(half + 1) * QE, :]

        def by_expert(t, q):
            return t[:, q, :].rearrange("p (e f) -> p e f", e=QE)

        def weights_of(q):
            t, half = q // HALVES, q % HALVES
            return wt[:, t, half * QE:(half + 1) * QE].unsqueeze(2).to_broadcast([P, QE, F])

        class Slots:
            in0, in1, silu, xp, xs, split, dt, pre, neg, c, cn, exp, one, ln, total, delta, du, b0 = \
                -1, 0, 1, 2, 3, 2, 3, 4, 4, 3, 5, 6, 6, 8, 8, 11, 12, 11

        class FirstSlots:
            in0, in1, silu, xp, xs, split, dt, pre, neg, c, cn, exp, one, ln, total, delta, du, b0 = \
                4, 5, 7, 8, 8, 7, 9, 9, 8, 9, 9, 10, 9, 11, 10, 11, 12, 11

        def p_bank(k):
            return pb[k % PB]

        def p_count(b, k):
            return P_USES * b + k // PB

        def f_bank(name):
            return F_ORDER.index(name) % FB

        def f_count(b, name):
            return F_USES * b + F_ORDER.index(name) // FB

        block = ctx.enter_context(nc.Block())

        @block.sync
        def _(sp_):
            sp_.dma_start(convw_sb[:, :, :].rearrange("p k e -> p (k e)"),
                          conv_w_t.partition_broadcast(P)).then_inc(ld_in, 16)
            sp_.dma_start(ctx_sb[:, 0:1, PAD:PAD + L], ctx_t[:, 0:1, :]).then_inc(ld_ctx0, 16)
            sp_.dma_start(wx_sb[:, :, :], w_x).then_inc(ld_wx, 16)
            sp_.dma_start(wdt_sb[DT0:DT0 + DR, :], w_dt_t).then_inc(ld_wx, 16)
            sp_.dma_start(ctx_sb[:, 1:B, PAD:PAD + L], ctx_t[:, 1:B, :]).then_inc(ld_ctx, 16)
            sp_.dma_start(router_sb[:, :, :], w_router).then_inc(ld_ffn, 16)
            sp_.dma_start(raw[:, :, :, :, :], w_gate_up).then_inc(ld_ffn, 16)
            sp_.dma_start(down_sb[:, :, :], w_down).then_inc(ld_down, 16)

            def store(b):
                sp_.wait_ge(out_ready, b + 1)
                sp_.dma_start(out[b].rearrange("(c p) e -> p c e", p=P), x_sb[:, b, :, :]).then_inc(out_stored, 16)

            with sp_.Fori(0, B) as b:
                store(b)
            sp_.wait_ge(out_stored, 16 * B)

        @block.gpsimd
        def _(gp):
            gp.memset(ctx_sb[:, :, 0:PAD], 0.0).then_inc(pad_ready, 1)

            def z_inv_std():
                gp.wait_ge(zchain, 3 * B * TC)
                gp.tensor_tensor(zrs[:, :, :].rearrange("p b c -> p (b c)"), zve[:, :],
                                 minus_half.to_broadcast([P, B * TC]), ALU.pow).then_inc(zrs_ready, 1)

            def skip_input(b):
                gp.wait_ge(p_read[IN], p_count(b, IN) + 1)
                gp.tensor_tensor(ud[:, :, :], u[:, :, :], dcol.unsqueeze(2).to_broadcast([P, EC, L]), ALU.mult)\
                  .then_inc(ud_ready, 1)

            def state_input(b, n, first):
                if n == 0:
                    gp.wait_ge(du_ready, b + 1)
                if n % 2 == 0:
                    k = BP + n // 2
                    gp.wait_ge(p_read[k % PB], p_count(b, k) + 1)
                if not first or n >= RING:
                    gp.wait_ge(scan_done, NS * b + n - RING + 1)
                gp.tensor_tensor(dbu[:, n % RING, :, :], du[:, :, :],
                                 b_all[:, n, :].unsqueeze(1).to_broadcast([P, EC, L]), ALU.mult)\
                  .then_inc(dbu_ready, 1)

            def low_weights(k):
                gp.wait_ge(whi_ready, k + 2)
                gp.tensor_tensor(piece(wlo, k), piece(raw, k), piece(whi, k).bitcast(fp32), ALU.subtract)\
                  .then_inc(wlo_ready, 1)

            def inv_std(b):
                gp.wait_ge(fchain, FCHAIN * b + FVAR)
                gp.tensor_tensor(frs[:, :], fve[:, :], minus_half.to_broadcast([P, TC]), ALU.pow)\
                  .then_inc(frs_ready, 1)

            def weigh(b, q):
                if q == 0:
                    gp.wait_ge(w_ready, b + 1)
                gp.wait_ge(gs_ready, NQ * b + q + 1)
                gp.tensor_tensor(by_expert(gs, q), by_expert(gs, q), weights_of(q), ALU.mult).then_inc(gw_ready, 1)

            def body(b, first, ffn, proj):
                for n in range(NS):
                    if n + LEAD < NS:
                        state_input(b, n + LEAD, first)
                    elif proj:
                        state_input(b + 1, n + LEAD - NS, False)
                    if first and 6 <= n < 6 + PIECES:
                        low_weights(n - 6)
                    if ffn and n == 2:
                        inv_std(b - 1)
                    if ffn and 8 <= n < 8 + NQ:
                        weigh(b - 1, n - 8)
                    if proj and n == 12:
                        skip_input(b + 1)

            gp.wait_ge(ld_col, 48)
            z_inv_std()
            skip_input(0)
            for n in range(LEAD):
                state_input(0, n, True)
            body(0, True, False, True)
            with gp.Fori(1, B - 1) as b:
                body(b, False, True, True)
            body(B - 1, False, True, False)
            inv_std(B - 1)

        @block.scalar
        def _(act):
            act.dma_start(win_sb[:, :], w_in_t).then_inc(ld_in, 16)
            act.dma_start(cols_sb[:, :], cols).then_inc(ld_col, 16)
            act.dma_start(consts_sb[:, :], consts).then_inc(ld_col, 16)
            act.dma_start(gains_sb[:, :], gains.partition_broadcast(P)).then_inc(ld_col, 16)
            act.dma_start(x_sb[:, :, :, :], x.rearrange("b (c p) e -> p b c e", p=P)).then_inc(ld_x, 16)

            def conv_silu(b, first):
                act.wait_ge(p_full[IN], p_count(b, IN) + 1)
                if not first:
                    act.wait_ge(du_ready, b)
                    act.wait_ge(ud_ready, b)
                for c in range(EC):
                    last = act.activation(u[:, c, :], p_bank(IN)[:, c * L:(c + 1) * L], ACT.Silu, bias=convb[:, c:c + 1])
                last.then_inc(p_read[IN], 1)

            def x_proj_out(b):
                act.wait_ge(p_full[XP % PB], p_count(b, XP) + 1)
                act.activation(xs[:, :], p_bank(XP)[0:XW, 0:L], ACT.Copy).then_inc(p_read[XP % PB], 1)
                act.wait_ge(p_read[XP % PB], p_count(b, XP) + 1)
                act.activation(part3[:, :], xs[0:DT0, :], ACT.Copy).then_inc(high_ready, 1)

            def dt_out(b):
                act.wait_ge(p_full[DT % PB], p_count(b, DT) + 1)
                for c in range(EC):
                    last = act.activation(pre[:, c, :], p_bank(DT)[:, c * L:(c + 1) * L], ACT.Identity,
                                          bias=dtb[:, c:c + 1])
                last.then_inc(p_read[DT % PB], 1)

            def c_out(b, first):
                act.wait_ge(p_full[CP % PB], p_count(b, CP) + 1)
                if not first:
                    act.wait_ge(c_ready, b)
                turned = p_bank(CP)[:, 0:TC * (XW - DT0)].rearrange("p (t k) -> p t k", t=TC)
                act.activation(c_next[:, :, :], turned[:, :, C0 - DT0:XW - DT0], ACT.Copy)\
                   .then_inc(p_read[CP % PB], 1)

            def softplus_exp(b):
                act.wait_ge(pchain, PCHAIN * b + 6)
                act.activation(texp[:, :, :], nabs[:, :, :], ACT.Exp).then_inc(texp_ready, 1)

            def softplus_ln(b):
                act.wait_ge(pchain, PCHAIN * b + 7)
                act.activation(tln[:, :, :], tp1[:, :, :], ACT.Ln).then_inc(tln_ready, 1)

            def b_out(b, j, first):
                k = BP + j
                act.wait_ge(p_full[k % PB], p_count(b, k) + 1)
                if not first:
                    act.wait_ge(dbu_ready, NS * (b - 1) + 2 * j + 2)
                act.activation(b_all[:, 2 * j:2 * j + 2, :].rearrange("p n l -> p (n l)"), p_bank(k)[:, :], ACT.Copy)\
                   .then_inc(p_read[k % PB], 1)

            def decay(b, n, first):
                if n == 0:
                    act.wait_ge(delta_ready, b + 1)
                if not first or n >= DA:
                    act.wait_ge(scan_done, NS * b + n - DA + 1)
                for c in range(EC):
                    last = act.activation(da[:, n % DA, c, 1:L], delta[:, c, 1:L], ACT.Exp, scale=a_neg[:, c, n:n + 1])
                last.then_inc(da_ready, 1)

            def skip_term(b, first):
                act.wait_ge(t_full, T_USES * b + 1)
                if not first:
                    act.wait_ge(t_read, T_USES * b)
                act.activation(acc[:, :, :].rearrange("p c e -> p (c e)"), tb[0][:, :], ACT.Copy)\
                   .then_inc(t_read, 1)

            def z_silu(b, first):
                if first:
                    act.wait_ge(zn_ready, 1)
                    act.wait_ge(ld_x, 16)
                else:
                    act.wait_ge(t_full, T_USES * b)
                for c in range(TC):
                    last = act.activation(sz[:, c, :], x_sb[:, b, c, :], ACT.Silu,
                                          bias=znm[:, b, c:c + 1], scale=zrs[:, b, c:c + 1])
                last.then_inc(sz_ready, 1)

            def high_weights(k):
                if k == 0:
                    act.wait_ge(ld_ffn, 32)
                    act.activation(rhi[:, :, :], router_sb[:, :, :], ACT.Copy).then_inc(whi_ready, 1)
                act.activation(piece(whi, k), piece(raw, k), ACT.Copy).then_inc(whi_ready, 1)

            def xn_high(b):
                act.wait_ge(o_full, O_USES * b + 1)
                act.activation(xhi[:, :, :].rearrange("p c l -> p (c l)"), ob[:, :], ACT.Copy).then_inc(xhi_ready, 1)

            def router_exp(b):
                act.wait_ge(fchain, FCHAIN * b + FVAR + 1)
                for c in range(TC):
                    last = act.activation(esc[:, c, :], sc[:, c, :], ACT.Exp, bias=smax[:, c:c + 1])
                last.then_inc(esc_ready, 1)

            def gate_silu(b, q):
                if q < NQ - 1:
                    k = f_bank(f"gate{q}")
                    act.wait_ge(f_full[k], f_count(b, f"gate{q}") + 1)
                    act.activation(gs[:, q, :], fb[k][:, :], ACT.Silu).then_inc(gs_ready, 1)
                else:
                    act.wait_ge(o_full, O_USES * b + 2)
                    act.activation(gs[:, q, :], ob[:, :], ACT.Silu).then_inc(gs_ready, 1)

            def hidden_out(b, q):
                k = f_bank(f"turn{q}")
                act.wait_ge(f_full[k], f_count(b, f"turn{q}") + 1)
                act.activation(hid_t[:, q, :], fb[k][:, :], ACT.Copy).then_inc(hidt_ready, 1)

            def body(b, first, ffn, proj):
                slot = FirstSlots if first else Slots
                for n in range(NS):
                    if n + LEAD < NS:
                        decay(b, n + LEAD, first)
                    elif proj:
                        decay(b + 1, n + LEAD - NS, False)
                    if first and n < 4:
                        b_out(b, n + NS // 4, True)
                    if n == 0:
                        skip_term(b, first)
                    if first and 4 <= n < 4 + PIECES:
                        high_weights(n - 4)
                    if n == slot.silu:
                        if proj:
                            conv_silu(b + 1, False)
                        z_silu(b, first)
                        act.preload_act_table_set(EXP_LN)
                    if proj and n == slot.xs:
                        x_proj_out(b + 1)
                    if ffn and n == 4:
                        xn_high(b - 1)
                    if proj and n == slot.pre:
                        dt_out(b + 1)
                    if ffn and n == 5:
                        router_exp(b - 1)
                    if proj and n == slot.cn:
                        c_out(b + 1, False)
                    if proj and n == slot.exp:
                        softplus_exp(b + 1)
                    if ffn and n == 7:
                        for q in range(NQ):
                            gate_silu(b - 1, q)
                        act.preload_act_table_set(EXP_LN)
                    if proj and n == slot.ln:
                        softplus_ln(b + 1)
                    if proj and slot.b0 <= n < slot.b0 + 4:
                        b_out(b + 1, 2 * (n - slot.b0), False)
                        b_out(b + 1, 2 * (n - slot.b0) + 1, False)
                    if ffn and 11 <= n < 11 + NQ:
                        hidden_out(b - 1, n - 11)

            act.wait_ge(ld_col, 48)
            act.activation(pick[:, :], pick_f, ACT.Copy).then_inc(pick_ready, 1)
            conv_silu(0, True)
            act.activation(tg[:, :], gains_sb[:, :], ACT.Tanh).then_inc(tanh_ready, 1)
            act.preload_act_table_set(EXP_LN)
            act.activation(a_exp[:, :], alog, ACT.Exp).then_inc(aexp_ready, 1)
            x_proj_out(0)
            dt_out(0)
            softplus_exp(0)
            c_out(0, True)
            softplus_ln(0)
            b_out(0, 0, True)
            act.wait_ge(a_ready, 2)
            for n in range(LEAD):
                decay(0, n, True)
            for j in range(1, NS // 4):
                b_out(0, j, True)
            body(0, True, False, True)
            with act.Fori(1, B - 1) as b:
                body(b, False, True, True)
            last_b = B - 1
            body(last_b, False, True, False)
            xn_high(last_b)
            router_exp(last_b)
            for q in range(NQ):
                gate_silu(last_b, q)
            for q in range(NQ):
                act.wait_ge(tail_turn, q + 1)
                act.activation(hid_t[:, q, :], tail_turns[q][:, :], ACT.Copy).then_inc(hidt_ready, 1)

        @block.vector
        def _(dve):
            def z_stats():
                for k in range(B * TC):
                    dve.bn_stats(zst[:, k, :], x_sb[:, k // TC, k % TC, :]).then_inc(zchain, 1)
                for k in range(B * TC):
                    dve.wait_ge(zchain, B * TC)
                    dve.bn_aggr(zmv[:, k, :], zst[:, k, :]).then_inc(zchain, 1)
                for k in range(B * TC):
                    dve.wait_ge(zchain, 2 * B * TC)
                    dve.tensor_scalar(zve[:, k:k + 1], zmv[:, k, 1:2], EPS, None, ALU.add).then_inc(zchain, 1)

            dve.memset(da[:, :, :, 0:1], 0.0).then_inc(a_ready, 1)

            dve.wait_ge(ld_in, 32)
            dve.tensor_tensor(wk_sb[:, :, :], convw_sb[:, :, :],
                              win_sb[:, :].unsqueeze(1).to_broadcast([P, TAPS, DI]), ALU.mult).then_inc(wk_ready, 1)
            dve.wait_ge(ld_x, 16)
            z_stats()
            dve.wait_ge(aexp_ready, 1)
            dve.tensor_scalar(a_neg[:, :, :].rearrange("p c n -> p (c n)"), a_exp[:, :], -1.0, None, ALU.mult)\
               .then_inc(a_ready, 1)

            def z_shift():
                dve.wait_ge(zrs_ready, 1)
                dve.scalar_tensor_tensor(znm[:, :, :].rearrange("p b c -> p (b c)"), zmv[:, :, 0], -1.0,
                                         zrs[:, :, :].rearrange("p b c -> p (b c)"), ALU.mult, ALU.mult)\
                   .then_inc(zn_ready, 1)

            def split_b(b):
                k = PCHAIN * b
                dve.wait_ge(high_ready, b + 1)
                dve.tensor_tensor(rest1[:, :], xs[0:DT0, :], part3[:, :], ALU.subtract).then_inc(pchain, 1)
                dve.wait_ge(pchain, k + 1)
                dve.tensor_copy(mid64[:, :], rest1[:, :]).then_inc(pchain, 1)
                dve.wait_ge(pchain, k + 2)
                dve.tensor_tensor(rest2[:, :], rest1[:, :], mid64[:, :], ALU.subtract).then_inc(pchain, 1)
                dve.tensor_copy(part3[32:64, :], mid64[32:64, :]).then_inc(pchain, 1)
                dve.wait_ge(pchain, k + 3)
                dve.tensor_copy(part3[64:96, :], rest2[64:96, :]).then_inc(pchain, 1)

            def softplus_abs(b):
                dve.wait_ge(p_read[DT % PB], p_count(b, DT) + 1)
                dve.scalar_tensor_tensor(flat(nabs), flat(pre), -1.0, flat(pre), ALU.mult, ALU.min)\
                   .then_inc(pchain, 1)

            def softplus_one(b):
                dve.wait_ge(texp_ready, b + 1)
                dve.tensor_scalar(flat(tp1), flat(texp), 1.0, None, ALU.add).then_inc(pchain, 1)

            def softplus_fix(b):
                dve.wait_ge(pchain, PCHAIN * b + 7)
                dve.scalar_tensor_tensor(flat(nfix), flat(tp1), -1.0, flat(texp), ALU.add, ALU.subtract)\
                   .then_inc(pchain, 1)

            def softplus_sum(b):
                dve.wait_ge(tln_ready, b + 1)
                dve.scalar_tensor_tensor(flat(sp), flat(pre), 0.0, flat(tln), ALU.max, ALU.add).then_inc(pchain, 1)

            def flat(t):
                return t[:, :, :].rearrange("p c l -> p (c l)")

            def take_delta(b, first):
                dve.wait_ge(pchain, PCHAIN * b + 9)
                if not first:
                    dve.wait_ge(da_ready, NS * b)
                dve.tensor_tensor(flat(delta), flat(sp), flat(nfix), ALU.subtract).then_inc(delta_ready, 1)

            def take_du(b, first):
                dve.wait_ge(delta_ready, b + 1)
                dve.wait_ge(p_read[IN], p_count(b, IN) + 1)
                if not first:
                    dve.wait_ge(dbu_ready, NS * b)
                dve.tensor_tensor(flat(du), flat(delta), flat(u), ALU.mult).then_inc(du_ready, 1)

            def take_c(b):
                dve.wait_ge(p_read[CP % PB], p_count(b, CP) + 1)
                dve.tensor_copy(c_t[:, :, :], c_next[:, :, :]).then_inc(c_ready, 1)

            def scan(b, n, first):
                dve.wait_ge(da_ready, NS * b + n + 1)
                dve.wait_ge(dbu_ready, NS * b + n + 1)
                if n >= RING:
                    dve.wait_ge(t_full, T_USES * b + n - RING + 2)
                elif not first:
                    dve.wait_ge(t_full, T_USES * (b - 1) + NS + n - RING + 2)
                dve.tensor_tensor_scan(h[:, n % RING, :, :].rearrange("p c l -> p (c l)"), da[:, n % DA, :, :].rearrange("p c l -> p (c l)"),
                                       dbu[:, n % RING, :, :].rearrange("p c l -> p (c l)"), 0.0,
                                       ALU.mult, ALU.add).then_inc(scan_done, 1)

            def add_state(b, n):
                dve.wait_ge(t_full, T_USES * b + n + 2)
                dve.wait_ge(t_read, T_USES * b + n + 1)
                if n == 0:
                    dve.wait_ge(c_ready, b + 1)
                src = tb[(n + 1) % 2]
                for c in range(TC):
                    last = dve.scalar_tensor_tensor(acc[:, c, :], src[:, c * DI:(c + 1) * DI], c_t[:, c, n:n + 1],
                                                    acc[:, c, :], ALU.mult, ALU.add)
                last.then_inc(t_read, 1)

            def gate_y(b):
                dve.wait_ge(t_full, T_USES * (b + 1))
                dve.wait_ge(t_read, T_USES * (b + 1) - 1)
                dve.tensor_tensor(flat(yg), tb[(NS + 1) % 2][:, :], flat(acc), ALU.mult).then_inc(t_read, 1)
                dve.wait_ge(t_read, T_USES * (b + 1))
                dve.scalar_tensor_tensor(flat(x1), flat(yg), tg[:, 0:1],
                                         x_sb[:, b, :, :].rearrange("p c e -> p (c e)"), ALU.mult, ALU.add)\
                   .then_inc(x1_ready, 1)

            def row_stats(b, last):
                k = FCHAIN * b
                dve.wait_ge(x1_ready, b + 1)
                for c in range(TC):
                    dve.bn_stats(fst[:, c, :], x1[:, c, :]).then_inc(fchain, 1)
                dve.wait_ge(fchain, k + TC)
                if not last:
                    take_c(b + 1)
                for c in range(TC):
                    dve.bn_aggr(fmv[:, c, :], fst[:, c, :]).then_inc(fchain, 1)
                dve.wait_ge(fchain, k + 2 * TC)
                dve.tensor_scalar(fve[:, :], fmv[:, :, 1], EPS, None, ALU.add).then_inc(fchain, 1)

            def normalise(b):
                dve.wait_ge(frs_ready, b + 1)
                for c in range(TC):
                    last = dve.tensor_scalar(xn[:, c, :], x1[:, c, :], fmv[:, c, 0:1], frs[:, c:c + 1],
                                             ALU.subtract, ALU.mult)
                last.then_inc(xn_ready, 1)

            def xn_low(b):
                dve.wait_ge(xhi_ready, b + 1)
                dve.tensor_tensor(flat(xlo), ob[:, :], flat(xhi).bitcast(fp32), ALU.subtract).then_inc(o_read, 1)

            def low_router():
                dve.wait_ge(whi_ready, 1)
                dve.tensor_tensor(rlo[:, :, :], router_sb[:, :, :], rhi[:, :, :].bitcast(fp32), ALU.subtract)\
                   .then_inc(wlo_ready, 1)

            def router_max(b):
                k = f_bank("scores")
                dve.wait_ge(f_full[k], f_count(b, "scores") + 1)
                dve.tensor_copy(sc[:, :, :].rearrange("p c e -> p (c e)"), fb[k][:, 0:TC * NE]).then_inc(sc_read, 1)
                dve.wait_ge(sc_read, b + 1)
                dve.tensor_reduce(smax[:, :], sc[:, :, :], mybir.AxisListType.X, ALU.max, negate=True)\
                   .then_inc(fchain, 1)

            def router_weights(b):
                k = FCHAIN * b + FVAR + 1
                for c in range(TC):
                    dve.max(top[:, c, :], esc[:, c, :]).then_inc(fchain, 1)
                dve.wait_ge(fchain, k + TC)
                dve.tensor_tensor(tsum[:, :], top[:, :, 0], top[:, :, 1], ALU.add)
                for c in range(TC):
                    last = dve.max_index(topi[:, c, :], top[:, c, :], esc[:, c, :])
                last.then_inc(fchain, 1)
                dve.wait_ge(fchain, k + TC + 1)
                dve.tensor_copy(topf[:, :, 0:2], topi[:, :, 0:2]).then_inc(fchain, 1)
                dve.reciprocal(trec[:, :], tsum[:, :])
                dve.wait_ge(fchain, k + TC + 2)
                for c in range(TC):
                    last = dve.tensor_scalar(hot1[:, c, :], iota, topf[:, c, 0:1], None, ALU.is_equal)
                last.then_inc(fchain, 1)
                dve.wait_ge(fchain, k + TC + 3)
                for c in range(TC):
                    last = dve.scalar_tensor_tensor(hot2[:, c, :], iota, topf[:, c, 1:2], hot1[:, c, :],
                                                    ALU.is_equal, ALU.add)
                last.then_inc(fchain, 1)
                dve.wait_ge(fchain, k + TC + 4)
                for c in range(TC):
                    last = dve.scalar_tensor_tensor(wt[:, c, :], esc[:, c, :], trec[:, c:c + 1], hot2[:, c, :],
                                                    ALU.mult, ALU.mult)
                last.then_inc(w_ready, 1)

            def hidden(b, q):
                k = f_bank(f"up{q}")
                dve.wait_ge(gw_ready, NQ * b + q + 1)
                dve.wait_ge(f_full[k], f_count(b, f"up{q}") + 1)
                dve.tensor_tensor(hid[:, q, :], fb[k][:, :], gs[:, q, :], ALU.mult).then_inc(hid_ready, 1)

            def weigh_direct(b, q):
                dve.wait_ge(gs_ready, NQ * b + q + 1)
                dve.tensor_tensor(by_expert(gs, q), by_expert(gs, q), weights_of(q), ALU.mult).then_inc(gw_ready, 1)

            def hidden_direct(b, q):
                dve.wait_ge(gw_ready, NQ * b + q + 1)
                dve.wait_ge(tail_up, q + 1)
                dve.tensor_tensor(hid[:, q, :], tail_ups[q][:, :], gs[:, q, :], ALU.mult).then_inc(hid_ready, 1)

            def finish(b, o_uses):
                dve.wait_ge(o_full, o_uses)
                dve.scalar_tensor_tensor(x_sb[:, b, :, :].rearrange("p c e -> p (c e)"), ob[:, :], tg[:, 1:2], flat(x1),
                                         ALU.mult, ALU.add).then_inc(out_ready, 1)

            def body(b, first, ffn, proj):
                slot = FirstSlots if first else Slots
                for n in range(NS):
                    if n + AHEAD < NS:
                        scan(b, n + AHEAD, first)
                    elif proj:
                        scan(b + 1, n + AHEAD - NS, False)
                    if ffn and n == 0:
                        row_stats(b - 1, False)
                    if ffn and n == 5:
                        dve.wait_ge(esc_ready, b)
                    add_state(b, n)
                    if first and n == 5:
                        low_router()
                    if ffn and n == 1:
                        normalise(b - 1)
                    if ffn and n == 2:
                        xn_low(b - 1)
                    if ffn and n == 3:
                        router_max(b - 1)
                    if ffn and n == 5:
                        router_weights(b - 1)
                    if proj and n == slot.split:
                        split_b(b + 1)
                    if ffn and 7 <= n < 7 + NQ:
                        hidden(b - 1, n - 7)
                    if proj and n == slot.neg:
                        softplus_abs(b + 1)
                    if proj and n == slot.one:
                        softplus_one(b + 1)
                        softplus_fix(b + 1)
                    if proj and n == slot.total:
                        softplus_sum(b + 1)
                    if proj and n == slot.delta:
                        take_delta(b + 1, False)
                    if proj and n == slot.du:
                        take_du(b + 1, False)
                if ffn:
                    finish(b - 1, O_USES * b)
                gate_y(b)

            split_b(0)
            softplus_abs(0)
            softplus_one(0)
            softplus_fix(0)
            softplus_sum(0)
            take_delta(0, True)
            take_du(0, True)
            take_c(0)
            z_shift()
            dve.wait_ge(tanh_ready, 1)
            for n in range(AHEAD):
                scan(0, n, True)
            body(0, True, False, True)
            with dve.Fori(1, B - 1) as b:
                body(b, False, True, True)
            body(B - 1, False, True, False)
            last_b = B - 1
            row_stats(last_b, True)
            normalise(last_b)
            xn_low(last_b)
            router_max(last_b)
            dve.wait_ge(esc_ready, B)
            router_weights(last_b)
            dve.wait_ge(w_ready, B)
            for q in range(NQ):
                weigh_direct(last_b, q)
            for q in range(NQ):
                hidden_direct(last_b, q)
            finish(last_b, O_USES * B)

        @block.tensor
        def _(pe):
            def in_proj(b, c, first):
                if first and c == 0:
                    pe.wait_ge(ld_ctx0, 16)
                    pe.wait_ge(pad_ready, 1)
                    pe.wait_ge(wk_ready, 1)
                elif c == 0:
                    pe.wait_ge(p_read[IN], p_count(b, IN))
                for k in range(TAPS):
                    last = pe.matmul(p_bank(IN)[:, c * L:(c + 1) * L], wk_sb[:, k, c * P:(c + 1) * P],
                                     ctx_sb[:, b, k:k + L], start=(k == 0), stop=(k == TAPS - 1))
                if c == EC - 1:
                    last.then_inc(p_full[IN], 1)

            def x_proj(b, first):
                pe.wait_ge(p_read[IN], p_count(b, IN) + 1)
                if first:
                    pe.wait_ge(ld_wx, 32)
                else:
                    pe.wait_ge(p_read[XP % PB], p_count(b, XP))
                for c in range(EC):
                    last = pe.matmul(p_bank(XP)[0:XW, 0:L], wx_sb[:, c, 0:XW], u[:, c, :], start=(c == 0),
                                     stop=(c == EC - 1))
                last.then_inc(p_full[XP % PB], 1)

            def dt_proj(b):
                pe.wait_ge(p_read[XP % PB], p_count(b, XP) + 1)
                pe.wait_ge(p_read[DT % PB], p_count(b, DT))
                for c in range(EC):
                    last = pe.matmul(p_bank(DT)[:, c * L:(c + 1) * L], wdt_sb[DT0:C0, c * P:(c + 1) * P],
                                     xs[DT0:C0, :], start=True, stop=True)
                last.then_inc(p_full[DT % PB], 1)

            def c_proj(b):
                for t in range(TC):
                    last = pe.transpose(p_bank(CP)[:, t * (XW - DT0):(t + 1) * (XW - DT0)],
                                        xs[DT0:XW, t * P:(t + 1) * P], ident[DT0:XW, DT0:XW])
                last.then_inc(p_full[CP % PB], 1)

            def b_spread(b, j, first):
                if j == 0:
                    pe.wait_ge(pchain, PCHAIN * b + 5)
                    if first:
                        pe.wait_ge(pick_ready, 1)
                k = BP + j
                pe.wait_ge(p_read[k % PB], p_count(b, k))
                for i in range(2):
                    n = 2 * j + i
                    last = pe.matmul(p_bank(k)[:, i * L:(i + 1) * L], pick[:, n:n + 1].to_broadcast([DT0, P]),
                                     part3[:, :], start=True, stop=True)
                last.then_inc(p_full[k % PB], 1)

            def skip_term(b, first):
                if first:
                    pe.wait_ge(ld_col, 48)
                else:
                    pe.wait_ge(t_read, T_USES * b - 1)
                pe.wait_ge(ud_ready, b + 1)
                for t in range(TC):
                    for c in range(EC):
                        o = t * DI + c * P
                        last = pe.transpose(tb[0][:, o:o + P], ud[:, c, t * P:(t + 1) * P], ident)
                last.then_inc(t_full, 1)

            def turn_state(b, n, first):
                pe.wait_ge(scan_done, NS * b + n + 1)
                if n >= 1:
                    pe.wait_ge(t_read, T_USES * b + n)
                elif not first:
                    pe.wait_ge(t_read, T_USES * b)
                for t in range(TC):
                    for c in range(EC):
                        o = t * DI + c * P
                        last = pe.transpose(tb[(n + 1) % 2][:, o:o + P], h[:, n % RING, c, t * P:(t + 1) * P], ident)
                last.then_inc(t_full, 1)

            def turn_z(b):
                pe.wait_ge(sz_ready, b + 1)
                pe.wait_ge(t_read, T_USES * b + NS)
                for t in range(TC):
                    for c in range(EC):
                        o = t * DI + c * P
                        last = pe.transpose(tb[(NS + 1) % 2][:, o:o + P], sz[:, c, t * P:(t + 1) * P], ident)
                last.then_inc(t_full, 1)

            def turn_xn(b):
                pe.wait_ge(xn_ready, b + 1)
                for c in range(EC):
                    for t in range(TC):
                        last = pe.transpose(ob[:, c * L + t * P:c * L + (t + 1) * P], xn[:, t, c * P:(c + 1) * P], ident)
                last.then_inc(o_full, 1)

            def three(out_ap, t, hi, lo, c):
                xh, xl = xhi[:, c, t * P:(t + 1) * P], xlo[:, c, t * P:(t + 1) * P]
                pe.matmul(out_ap, xh, hi, start=(c == 0), stop=False)
                pe.matmul(out_ap, xh, lo, start=False, stop=False)
                return pe.matmul(out_ap, xl, hi, start=False, stop=(c == EC - 1))

            def router(b):
                pe.wait_ge(xhi_ready, b + 1)
                pe.wait_ge(o_read, O_READS * b + 1)
                k = f_bank("scores")
                for t in range(TC):
                    for c in range(EC):
                        last = three(fb[k][:, t * NE:(t + 1) * NE], t, rhi[:, c, :], rlo[:, c, :], c)
                last.then_inc(f_full[k], 1)

            def quarter(dst, q, what):
                t, half = q // HALVES, q % HALVES
                for c in range(EC):
                    k = (c * 2 + what) * HALVES + half
                    last = three(dst[:, :], t, piece(whi, k).rearrange("p e f -> p (e f)"),
                                 piece(wlo, k).rearrange("p e f -> p (e f)"), c)
                return last

            def gates(b, q):
                if q < NQ - 1:
                    k = f_bank(f"gate{q}")
                    if q == 2:
                        pe.wait_ge(sc_read, b + 1)
                    quarter(fb[k], q, 0).then_inc(f_full[k], 1)
                else:
                    quarter(ob, q, 0).then_inc(o_full, 1)

            def ups(b, q):
                k = f_bank(f"up{q}")
                if q < NQ - 1:
                    pe.wait_ge(gs_ready, NQ * b + q + 1)
                else:
                    pe.wait_ge(hid_ready, NQ * b + 2)
                quarter(fb[k], q, 1).then_inc(f_full[k], 1)

            def turn(dst, q):
                for e in range(QE):
                    last = pe.transpose(dst[:, e * P:(e + 1) * P], hid[:, q, e * F:(e + 1) * F], ident)
                return last

            def turn_hidden(b, q):
                k = f_bank(f"turn{q}")
                if q == 0:
                    pe.wait_ge(hid_ready, NQ * b + 1)
                elif q == 1:
                    pe.wait_ge(hid_ready, NQ * b + 3)
                elif q == 2:
                    pe.wait_ge(hidt_ready, NQ * b + 1)
                else:
                    pe.wait_ge(hid_ready, NQ * b + 4)
                turn(fb[k], q).then_inc(f_full[k], 1)

            def downs(b, q):
                if q == 0:
                    pe.wait_ge(gs_ready, NQ * (b + 1))
                pe.wait_ge(hidt_ready, NQ * b + q + 1)
                t, half = q // HALVES, q % HALVES
                for e in range(QE):
                    last = pe.matmul(ob[:, t * DI:(t + 1) * DI], hid_t[:, q, e * P:(e + 1) * P],
                                     down_sb[:, half * QE + e, :], start=(half == 0 and e == 0),
                                     stop=(half == HALVES - 1 and e == QE - 1))
                if q == NQ - 1:
                    last.then_inc(o_full, 1)

            def body(b, first, ffn, proj):
                slot = FirstSlots if first else Slots
                if proj and slot.in0 < 0:
                    in_proj(b + 1, 0, False)
                for n in range(NS):
                    turn_state(b, n, first)
                    if first and n < NS // 4:
                        b_spread(b, n + NS // 4, True)
                    if proj and n == slot.in0:
                        in_proj(b + 1, 0, False)
                    if proj and n == slot.in1:
                        in_proj(b + 1, 1, False)
                    if ffn and n == 3:
                        turn_xn(b - 1)
                    if proj and n == slot.xp:
                        x_proj(b + 1, False)
                    if proj and n == slot.dt:
                        dt_proj(b + 1)
                        c_proj(b + 1)
                    if ffn and n == 4:
                        router(b - 1)
                    if ffn and n in (5, 6):
                        gates(b - 1, 2 * (n - 5))
                        gates(b - 1, 2 * (n - 5) + 1)
                    if ffn and n in (8, 9, 10):
                        ups(b - 1, n - 8)
                    if ffn and n == 10:
                        turn_hidden(b - 1, 0)
                    if proj and slot.b0 <= n < slot.b0 + 4:
                        b_spread(b + 1, 2 * (n - slot.b0), False)
                        b_spread(b + 1, 2 * (n - slot.b0) + 1, False)
                    if ffn and n == 11:
                        ups(b - 1, 3)
                    if ffn and 12 <= n < 12 + NQ:
                        if n < 15:
                            turn_hidden(b - 1, n - 11)
                        downs(b - 1, n - 12)
                turn_z(b)
                if proj:
                    skip_term(b + 1, False)

            in_proj(0, 0, True)
            in_proj(0, 1, True)
            x_proj(0, True)
            dt_proj(0)
            c_proj(0)
            for j in range(NS // 4):
                b_spread(0, j, True)
            skip_term(0, True)
            pe.wait_ge(ld_ctx, 16)
            body(0, True, False, True)
            pe.wait_ge(wlo_ready, PIECES + 1)
            pe.wait_ge(ld_down, 16)
            with pe.Fori(1, B - 1) as b:
                body(b, False, True, True)
            last_b = B - 1
            body(last_b, False, True, False)
            turn_xn(last_b)
            router(last_b)
            for q in range(NQ):
                gates(last_b, q)
            for q in range(NQ):
                quarter(tail_ups[q], q, 1).then_inc(tail_up, 1)
            for q in range(NQ):
                pe.wait_ge(gs_ready, NQ * last_b + q + 1)
                pe.wait_ge(hid_ready, NQ * last_b + q + 1)
                turn(tail_turns[q], q).then_inc(tail_turn, 1)
                if q >= 1:
                    downs(last_b, q - 1)
            downs(last_b, NQ - 1)


def kernel(x, ctx_1024, g_xattn, g_ffn, L0_xattn_in_proj_w, L0_xattn_conv_w, L0_xattn_conv_b, L0_xattn_x_proj_w,
           L0_xattn_dt_proj_w, L0_xattn_dt_proj_b, L0_xattn_A_log, L0_xattn_D, L0_ffn_router_w, L0_ffn_gate_proj,
           L0_ffn_up_proj, L0_ffn_down_proj):
    import numpy as np
    import concourse.bacc as bacc
    from concourse.bass_utils import run_bass_kernel_spmd

    P = 128

    def arr(a):
        return np.asarray(a)

    def by_partition(a):
        a = arr(a)
        return np.swapaxes(a.reshape((a.shape[0] // P, P) + a.shape[1:]), 0, 1)

    xw = arr(L0_xattn_x_proj_w)
    ns = arr(L0_xattn_A_log).shape[1]
    dr = arr(L0_xattn_dt_proj_w).shape[1]
    dt_rows, b_rows, c_rows = xw[:dr], xw[dr:dr + ns], xw[dr + ns:]
    gap = np.zeros((32 - ns, xw.shape[1]), xw.dtype)
    w_x = np.concatenate([b_rows, gap, b_rows, gap, b_rows, gap, dt_rows, c_rows], 0).T
    ne = arr(L0_ffn_router_w).shape[1]
    consts = np.zeros((P, P + 32 + ne + 1), np.float32)
    consts[:, :P] = np.eye(P)
    consts[:, P:P + 32] = np.tile(np.eye(32), (P // 32, 1))
    consts[:, P + 32:P + 32 + ne] = np.arange(ne)
    consts[:, P + 32 + ne] = -0.5
    data = {
        "x": arr(x),
        "ctx_t": np.transpose(arr(ctx_1024), (2, 0, 1)),
        "w_in_t": arr(L0_xattn_in_proj_w).T,
        "conv_w_t": arr(L0_xattn_conv_w).T.reshape(-1),
        "cols": np.concatenate([by_partition(L0_xattn_conv_b), by_partition(L0_xattn_dt_proj_b),
                                by_partition(L0_xattn_D), by_partition(L0_xattn_A_log).reshape(P, -1)], 1),
        "w_x": by_partition(w_x),
        "w_dt_t": arr(L0_xattn_dt_proj_w).T,
        "w_router": by_partition(L0_ffn_router_w),
        "w_gate_up": np.transpose(np.stack([arr(L0_ffn_gate_proj), arr(L0_ffn_up_proj)], 1)
                                  .reshape(ne, 2, -1, P, P), (3, 2, 1, 0, 4)),
        "w_down": np.transpose(arr(L0_ffn_down_proj), (1, 0, 2)),
        "gains": np.concatenate([arr(g_xattn), arr(g_ffn)]),
        "consts": consts,
    }
    nc = bacc.Bacc("TRN2", target_bir_lowering=False, num_devices=1)
    arrays, args = {}, {}
    for name, a in data.items():
        a = np.ascontiguousarray(a)
        arrays[f"in_{name}"] = a
        args[name] = nc.dram_tensor(f"in_{name}", a.shape, mybir.dt.from_np(a.dtype), kind="ExternalInput").ap()
    out = nc.dram_tensor("out", data["x"].shape, mybir.dt.float32, kind="ExternalOutput").ap()
    mamba_moe_program(nc, out=out, **args)
    r = run_bass_kernel_spmd(nc, [arrays], core_ids=[0])
    return r.results[0]["out"]
```

```python
import concourse.bass as bass
from concourse import mybir
from contextlib import ExitStack



def mamba_moe_program(nc, x, ctx_t, w_in_t, conv_w_t, cols, w_x, w_dt_t, w_router, w_gate_up, w_down,
                      gains, consts, out):
    fp32 = mybir.dt.float32
    bf16 = mybir.dt.bfloat16
    fp32r = mybir.dt.float32r
    u32 = mybir.dt.uint32
    ALU = mybir.AluOpType
    ACT = mybir.ActivationFunctionType

    P = 128
    B, L, DI = x.shape
    EC = DI // P
    TC = L // P
    DM = ctx_t.shape[0]
    TAPS = conv_w_t.shape[0] // DI
    NS = 16
    NE = w_router.shape[2]
    F = w_down.shape[0]
    DR = w_dt_t.shape[0]
    DT0 = 96
    C0 = DT0 + DR
    XW = C0 + NS
    PAD = TAPS - 1
    EPS = 1e-5
    assert EC == 2 and TC == 2 and DM == P and F == P and EC * L == 512

    T_USES = NS + 2
    PB = 2
    P_USES = (4 + NS // 2) // PB
    F_BANKS = [["scores", "gate2", "turn0", "turn1"],
               ["gate0", "up2", "turn2"],
               ["gate1", "up3", "turn3"]]
    FB = len(F_BANKS)
    O_USES = 3
    O_READS = 1
    RING = 8
    HR = 4
    DA = 8
    LEAD = 4
    DLEAD = 4
    AHEAD = 2
    QE = 512 // F
    HALVES = NE // QE
    NQ = TC * HALVES

    PCHAIN = 9
    FCHAIN = 12
    FVAR = 5

    ctx = ExitStack()
    with ctx:
        def sb(name, shape, dt=fp32):
            return ctx.enter_context(nc.sbuf_tensor(name, shape, dt))

        def bank(name):
            return ctx.enter_context(nc.psum_tensor(name, [P, 512], fp32))

        def sem(name):
            return ctx.enter_context(nc.semaphore(name))

        x_sb = sb("x_sb", [P, B, TC, DI])
        ctx_sb = sb("ctx_sb", [P, B, PAD + L])
        win_sb = sb("win_sb", [P, DI])
        convw_sb = sb("convw_sb", [P, TAPS, DI])
        wk_sb = sb("wk_sb", [P, TAPS, DI])
        wk_hi = sb("wk_hi", [P, TAPS, DI], fp32r)
        wk_lo = sb("wk_lo", [P, TAPS, DI], fp32r)
        ctx_hi = sb("ctx_hi", [P, B, PAD + L], fp32r)
        ctx_lo = sb("ctx_lo", [P, B, PAD + L], fp32r)
        cols_sb = sb("cols_sb", [P, 3 * EC + EC * NS])
        convb = cols_sb[:, 0:EC]
        dtb = cols_sb[:, EC:2 * EC]
        dcol = cols_sb[:, 2 * EC:3 * EC]
        alog = cols_sb[:, 3 * EC:3 * EC + EC * NS]
        a_exp = sb("a_exp", [P, EC * NS])
        a_neg = sb("a_neg", [P, EC, NS])
        wx_sb = sb("wx_sb", [P, EC, XW])
        wdt_sb = sb("wdt_sb", [P, DI])
        router_sb = sb("router_sb", [P, EC, NE])
        raw = sb("raw", [P, EC, 2, NE, F])
        rhi = sb("rhi", [P, EC, NE], fp32r)
        rlo = sb("rlo", [P, EC, NE], fp32r)
        whi = sb("whi", [P, EC, 2, NE, F], fp32r)
        wlo = sb("wlo", [P, EC, 2, NE, F], fp32r)
        down_sb = sb("down_sb", [P, NE, DI])
        gains_sb = sb("gains_sb", [P, 2])
        tg = sb("tg", [P, 2])
        consts_sb = sb("consts_sb", [P, P + 32 + NE + 1])
        ident = consts_sb[:, 0:P]
        pick_f = consts_sb[0:DT0, P:P + 32]
        iota = consts_sb[:, P + 32:P + 32 + NE]
        minus_half = consts_sb[:, P + 32 + NE:P + 32 + NE + 1]
        pick = sb("pick", [DT0, 32], bf16)

        zst = sb("zst", [P, B * TC, 6])
        zmv = sb("zmv", [P, B * TC, 2])
        zve = sb("zve", [P, B * TC])
        zrs = sb("zrs", [P, B, TC])
        znm = sb("znm", [P, B, TC])
        sz = sb("sz", [P, TC, L])

        u = sb("u", [P, EC, L])
        ud = sb("ud", [P, EC, L])
        xs = sb("xs", [XW, L])
        part3 = sb("part3", [DT0, L], bf16)
        rest1 = sb("rest1", [DT0, L])
        mid64 = sb("mid64", [DT0, L], bf16)
        rest2 = sb("rest2", [DT0, L])
        pre = sb("pre", [P, EC, L])
        texp = sb("texp", [P, EC, L])
        tp1 = sb("tp1", [P, EC, L])
        tln = sb("tln", [P, EC, L])
        nfix = sb("nfix", [P, EC, L])
        sp = sb("sp", [P, EC, L])
        c_next = sb("c_next", [P, TC, NS])
        b_all = sb("b_all", [P, NS, L])

        delta = sb("delta", [P, EC, L])
        du = sb("du", [P, EC, L])
        c_t = sb("c_t", [P, TC, NS])
        da = sb("da", [P, DA, EC, L])
        dbu = sb("dbu", [P, RING, EC, L])
        h = sb("h", [P, HR, EC, L])
        acc = sb("acc", [P, TC, DI])
        yg = sb("yg", [P, TC, DI])

        fst = sb("fst", [P, TC, 6])
        fmv = sb("fmv", [P, TC, 2])
        fve = sb("fve", [P, TC])
        frs = sb("frs", [P, TC])
        xn = sb("xn", [P, TC, DI])
        xhi = sb("xhi", [P, EC, L], fp32r)
        xlo = sb("xlo", [P, EC, L], fp32r)
        sc = sb("sc", [P, TC, NE])
        smax = sb("smax", [P, TC])
        esc = sb("esc", [P, TC, NE])
        top = sb("top", [P, TC, 8])
        topi = sb("topi", [P, TC, 8], u32)
        topf = sb("topf", [P, TC, 8])
        tsum = sb("tsum", [P, TC])
        trec = sb("trec", [P, TC])
        hot1 = sb("hot1", [P, TC, NE])
        hot2 = sb("hot2", [P, TC, NE])
        wt = sb("wt", [P, TC, NE])
        gs = sb("gs", [P, NQ, QE * F])
        hid_t = sb("hid_t", [P, NQ, QE * P])

        tb = [bank("tb0"), bank("tb1")]
        pb = [bank(f"pb{k}") for k in range(PB)]
        fb = [bank(f"fb{k}") for k in range(FB)]
        ob = bank("ob")

        ld_ctx0, ld_ctx, ld_in, ld_x, ld_col = sem("ld_ctx0"), sem("ld_ctx"), sem("ld_in"), sem("ld_x"), sem("ld_col")
        ld_wx, ld_ffn, ld_down = sem("ld_wx"), sem("ld_ffn"), sem("ld_down")
        wk_made, ctx_hi_ready, ctx_ready = sem("wk_made"), sem("ctx_hi_ready"), sem("ctx_ready")
        pad_ready, wk_ready, pick_ready = sem("pad_ready"), sem("wk_ready"), sem("pick_ready")
        aexp_ready, a_ready, tanh_ready = sem("aexp_ready"), sem("a_ready"), sem("tanh_ready")
        whi_ready, wlo_ready = sem("whi_ready"), sem("wlo_ready")
        zchain, zrs_ready, zn_ready = sem("zchain"), sem("zrs_ready"), sem("zn_ready")
        p_full = [sem(f"p_full{k}") for k in range(PB)]
        p_read = [sem(f"p_read{k}") for k in range(PB)]
        high_ready, pchain, texp_ready, tln_ready = sem("high_ready"), sem("pchain"), sem("texp_ready"), sem("tln_ready")
        head_act, head_dve = sem("head_act"), sem("head_dve")
        delta_ready, du_ready, c_ready = sem("delta_ready"), sem("du_ready"), sem("c_ready")
        da_ready, dbu_ready, scan_done = sem("da_ready"), sem("dbu_ready"), sem("scan_done")
        t_full, t_read, sz_ready, x1_ready = sem("t_full"), sem("t_read"), sem("sz_ready"), sem("x1_ready")
        fchain, frs_ready, xn_ready, esc_ready = sem("fchain"), sem("frs_ready"), sem("xn_ready"), sem("esc_ready")
        xhi_ready, ud_ready, w_ready = sem("xhi_ready"), sem("ud_ready"), sem("w_ready")
        early_full = sem("early_full")
        f_full = [sem(f"f_full{k}") for k in range(FB)]
        sc_read = sem("sc_read")
        o_full, o_read = sem("o_full"), sem("o_read")
        gs_ready, gw_ready, hid_ready, hidt_ready = sem("gs_ready"), sem("gw_ready"), sem("hid_ready"), sem("hidt_ready")
        tail_full = sem("tail_full")
        T_XN, T_GATE, T_UP, T_TURN = 1, 1 + TC, 1 + TC + NQ, 1 + TC + 2 * NQ
        out_ready, out_stored = sem("out_ready"), sem("out_stored")

        tail_xn = [tb[0], fb[0]]
        tail_gates = [fb[1], fb[2], pb[0], pb[1]]
        tail_ups = [tb[1], tb[0], fb[0], fb[1]]
        tail_turns = [fb[2], pb[0], pb[1], tb[1]]
        tail_sums = [ob, fb[0]]
        EXP_LN = "natural_log_exp_and_others"

        IN, XP, DT, CP, BP = 0, 1, 2, 3, 4

        PIECES = EC * 2 * HALVES

        def piece(t, k):
            c, what, half = k // (2 * HALVES), k // HALVES % 2, k % HALVES
            return t[:, c, what, half * QE:(half + 1) * QE, :]

        def by_chunk(bank):
            return bank[:, 0:EC * P].rearrange("p (c l) -> p c l", c=EC)

        def by_expert(t, q):
            return t[:, q, :].rearrange("p (e f) -> p e f", e=QE)

        def weights_of(q):
            t, half = q // HALVES, q % HALVES
            return wt[:, t, half * QE:(half + 1) * QE].unsqueeze(2).to_broadcast([P, QE, F])

        FIRST = {
            "skip": 11, "delta": 11,
            "silu": 5, "xs": 5, "pre": 8, "c_next": 8, "exp": 9, "ln": 10,
            "b_all": [9, 9, 10, 10, 11, 11, 12, 13],
            "split": 7, "neg": 8, "one": 9, "sum": 10, "du": 11,
            "in": [3, 5], "x_proj": 8, "dt": 8, "b": [8, 8, 10, 10, 11, 11, 12, 12],
        }
        MIDDLE = {
            "inv": 1, "weigh": [7, 7, 7, 9], "skip": 11, "delta": 11,
            "xhi": 2, "silu": 2, "xs": 5, "esc": 4, "pre": 7, "c_next": 7, "exp": 8, "gate_silu": 7,
            "ln": 10, "hid_t": [11, 12, 12, 13], "b_all": [12, 12, 13, 13, 14, 14, 15, 15],
            "xn": 0, "xlo": 1, "smax": 3, "top": 4, "split": 5, "neg": 6, "one": 8,
            "hid": [7, 7, 8, 10], "sum": 9, "du": 11,
            "in": [0, 1], "turn_xn": 0, "router": 3, "gate": [4, 5, 6, 6], "up": [7, 8, 9, 9],
            "turn": [10, 10, 11, 12], "down": [10, 10, 13, 13, 14, 14, 15, 16], "x_proj": 5, "dt": 6,
            "b": [12, 12, 13, 13, 14, 14, 15, 15],
        }
        LAST = {
            "inv": 1, "weigh": [7, 8, 9, 10],
            "xhi": 3, "silu": 4, "esc": 7, "gate_silu": 8, "hid_t": [11, 12, 12, 13],
            "xn": 0, "xlo": 1, "smax": 4, "top": 5, "hid": [7, 7, 8, 9],
            "turn_xn": 1, "router": 3, "gate": [4, 5, 6, 6], "up": [6, 7, 8, 9],
            "turn": [8, 9, 10, 12], "down": [11, 12, 13, 14, 16, 16, 16, 16],
        }

        def p_bank(k):
            return pb[k % PB]

        def p_count(b, k):
            return P_USES * b + k // PB

        def f_bank(name):
            return [k for k in range(FB) if name in F_BANKS[k]][0]

        def f_count(b, name):
            uses = F_BANKS[f_bank(name)]
            return len(uses) * b + uses.index(name)

        block = ctx.enter_context(nc.Block())

        @block.sync
        def _(sp_):
            sp_.dma_start(convw_sb[:, :, :].rearrange("p k e -> p (k e)"),
                          conv_w_t.partition_broadcast(P)).then_inc(ld_in, 16)
            sp_.dma_start(ctx_sb[:, 0:1, PAD:PAD + L], ctx_t[:, 0:1, :]).then_inc(ld_ctx0, 16)
            sp_.dma_start(wx_sb[:, :, :], w_x).then_inc(ld_wx, 16)
            sp_.dma_start(wdt_sb[DT0:DT0 + DR, :], w_dt_t).then_inc(ld_wx, 16)
            sp_.dma_start(ctx_sb[:, 1:B, PAD:PAD + L], ctx_t[:, 1:B, :]).then_inc(ld_ctx, 16)
            sp_.dma_start(router_sb[:, :, :], w_router).then_inc(ld_ffn, 16)
            sp_.dma_start(raw[:, :, :, :, :], w_gate_up).then_inc(ld_ffn, 16)
            sp_.dma_start(down_sb[:, :, :], w_down).then_inc(ld_down, 16)

            def store(b):
                sp_.wait_ge(out_ready, b + 1)
                sp_.dma_start(out[b].rearrange("(c p) e -> p c e", p=P), x_sb[:, b, :, :]).then_inc(out_stored, 16)

            with sp_.Fori(0, B - 1) as b:
                store(b)
            for t in range(TC):
                sp_.wait_ge(out_ready, B + t)
                sp_.dma_start(out[B - 1, t * P:(t + 1) * P, :], x_sb[:, B - 1, t, :]).then_inc(out_stored, 16)
            sp_.wait_ge(out_stored, 16 * (B - 1 + TC))

        @block.gpsimd
        def _(gp):
            gp.memset(ctx_sb[:, :, 0:PAD], 0.0).then_inc(pad_ready, 1)

            def split_ctx(k, rows):
                gp.tensor_copy(ctx_hi[:, rows, :], ctx_sb[:, rows, :]).then_inc(ctx_hi_ready, 1)
                gp.wait_ge(ctx_hi_ready, k + 1)
                gp.tensor_tensor(ctx_lo[:, rows, :], ctx_sb[:, rows, :], ctx_hi[:, rows, :].bitcast(fp32), ALU.subtract)\
                  .then_inc(ctx_ready, 1)

            def z_inv_std():
                gp.wait_ge(zchain, 3 * B * TC)
                gp.tensor_tensor(zrs[:, :, :].rearrange("p b c -> p (b c)"), zve[:, :],
                                 minus_half.to_broadcast([P, B * TC]), ALU.pow).then_inc(zrs_ready, 1)

            def skip_input(b):
                gp.wait_ge(p_read[IN], p_count(b, IN) + 1)
                gp.tensor_tensor(ud[:, :, :], u[:, :, :], dcol.unsqueeze(2).to_broadcast([P, EC, L]), ALU.mult)\
                  .then_inc(ud_ready, 1)

            def state_input(b, n, first):
                if n == 0:
                    gp.wait_ge(du_ready, b + 1)
                if n % 2 == 0:
                    k = BP + n // 2
                    gp.wait_ge(p_read[k % PB], p_count(b, k) + 1)
                if not first or n >= RING:
                    gp.wait_ge(scan_done, NS * b + n - RING + 1)
                gp.tensor_tensor(dbu[:, n % RING, :, :], du[:, :, :],
                                 b_all[:, n, :].unsqueeze(1).to_broadcast([P, EC, L]), ALU.mult)\
                  .then_inc(dbu_ready, 1)

            def low_weights(k):
                gp.wait_ge(whi_ready, k + 2)
                gp.tensor_tensor(piece(wlo, k), piece(raw, k), piece(whi, k).bitcast(fp32), ALU.subtract)\
                  .then_inc(wlo_ready, 1)

            def take_delta(b):
                gp.wait_ge(pchain, PCHAIN * b + 9)
                gp.wait_ge(da_ready, NS * b)
                gp.tensor_tensor(delta[:, :, :], sp[:, :, :], nfix[:, :, :], ALU.subtract).then_inc(delta_ready, 1)

            def inv_std(b):
                gp.wait_ge(fchain, FCHAIN * b + FVAR)
                gp.tensor_tensor(frs[:, :], fve[:, :], minus_half.to_broadcast([P, TC]), ALU.pow)\
                  .then_inc(frs_ready, 1)

            def weigh(b, q):
                if q == 0:
                    gp.wait_ge(w_ready, b + 1)
                gp.wait_ge(gs_ready, NQ * b + q + 1)
                gp.tensor_tensor(by_expert(gs, q), by_expert(gs, q), weights_of(q), ALU.mult).then_inc(gw_ready, 1)

            def body(b, slot, first, ffn, proj):
                for n in range(NS):
                    if n + LEAD < NS:
                        state_input(b, n + LEAD, first)
                    elif proj:
                        state_input(b + 1, n + LEAD - NS, False)
                    if first and 6 <= n < 6 + PIECES:
                        low_weights(n - 6)
                    if ffn and n == slot["inv"]:
                        inv_std(b - 1)
                    if proj and n == slot["delta"]:
                        take_delta(b + 1)
                    for q in range(NQ):
                        if ffn and n == slot["weigh"][q]:
                            weigh(b - 1, q)
                    if proj and n == slot["skip"]:
                        skip_input(b + 1)

            gp.wait_ge(pad_ready, 1)
            gp.wait_ge(ld_ctx0, 16)
            split_ctx(0, slice(0, 1))
            gp.wait_ge(ld_ctx, 16)
            split_ctx(1, slice(1, B))
            gp.wait_ge(ld_col, 48)
            z_inv_std()
            skip_input(0)
            gp.wait_ge(p_read[BP % PB], p_count(0, BP) + 1)
            gp.wait_ge(head_dve, 6)
            gp.tensor_tensor(dbu[:, 0, 0, :], du[:, 0, :], b_all[:, 0, :], ALU.mult)
            gp.wait_ge(du_ready, 1)
            gp.tensor_tensor(dbu[:, 0, 1, :], du[:, 1, :], b_all[:, 0, :], ALU.mult).then_inc(dbu_ready, 1)
            for n in range(1, LEAD):
                state_input(0, n, True)
            body(0, FIRST, True, False, True)
            with gp.Fori(1, B - 1) as b:
                body(b, MIDDLE, False, True, True)
            body(B - 1, LAST, False, True, False)
            inv_std(B - 1)

        @block.scalar
        def _(act):
            act.dma_start(win_sb[:, :], w_in_t).then_inc(ld_in, 16)
            act.dma_start(cols_sb[:, :], cols).then_inc(ld_col, 16)
            act.dma_start(consts_sb[:, :], consts).then_inc(ld_col, 16)
            act.dma_start(gains_sb[:, :], gains.partition_broadcast(P)).then_inc(ld_col, 16)
            act.dma_start(x_sb[:, :, :, :], x.rearrange("b (c p) e -> p b c e", p=P)).then_inc(ld_x, 16)

            def conv_silu(b, first):
                act.wait_ge(p_full[IN], p_count(b, IN) + 1)
                if not first:
                    act.wait_ge(du_ready, b)
                    act.wait_ge(ud_ready, b)
                for c in range(EC):
                    last = act.activation(u[:, c, :], p_bank(IN)[:, c * L:(c + 1) * L], ACT.Silu, bias=convb[:, c:c + 1])
                last.then_inc(p_read[IN], 1)

            def x_proj_out(b):
                act.wait_ge(p_full[XP % PB], p_count(b, XP) + 1)
                act.activation(xs[:, :], p_bank(XP)[0:XW, 0:L], ACT.Copy).then_inc(p_read[XP % PB], 1)
                act.wait_ge(p_read[XP % PB], p_count(b, XP) + 1)
                act.activation(part3[:, :], xs[0:DT0, :], ACT.Copy).then_inc(high_ready, 1)

            def dt_out(b):
                act.wait_ge(p_full[DT % PB], p_count(b, DT) + 1)
                for c in range(EC):
                    last = act.activation(pre[:, c, :], p_bank(DT)[:, c * L:(c + 1) * L], ACT.Identity,
                                          bias=dtb[:, c:c + 1])
                last.then_inc(p_read[DT % PB], 1)

            def c_out(b, first):
                act.wait_ge(p_full[CP % PB], p_count(b, CP) + 1)
                if not first:
                    act.wait_ge(c_ready, b)
                turned = p_bank(CP)[:, 0:TC * (XW - DT0)].rearrange("p (t k) -> p t k", t=TC)
                act.activation(c_next[:, :, :], turned[:, :, C0 - DT0:XW - DT0], ACT.Copy)\
                   .then_inc(p_read[CP % PB], 1)

            def softplus_exp(b):
                act.wait_ge(pchain, PCHAIN * b + 6)
                act.activation(texp[:, :, :], texp[:, :, :], ACT.Exp).then_inc(texp_ready, 1)

            def softplus_ln(b):
                act.wait_ge(pchain, PCHAIN * b + 7)
                act.activation(tln[:, :, :], tp1[:, :, :], ACT.Ln).then_inc(tln_ready, 1)

            def b_out(b, j, first):
                k = BP + j
                act.wait_ge(p_full[k % PB], p_count(b, k) + 1)
                if not first:
                    act.wait_ge(dbu_ready, NS * (b - 1) + 2 * j + 2)
                act.activation(b_all[:, 2 * j:2 * j + 2, :].rearrange("p n l -> p (n l)"), p_bank(k)[:, :], ACT.Copy)\
                   .then_inc(p_read[k % PB], 1)

            def decay(b, n, first):
                if n == 0:
                    act.wait_ge(delta_ready, b + 1)
                if not first or n >= DA:
                    act.wait_ge(scan_done, NS * b + n - DA + 1)
                for c in range(EC):
                    last = act.activation(da[:, n % DA, c, 1:L], delta[:, c, 1:L], ACT.Exp, scale=a_neg[:, c, n:n + 1])
                last.then_inc(da_ready, 1)

            def skip_term(b, first):
                act.wait_ge(t_full, T_USES * b + 1)
                if not first:
                    act.wait_ge(t_read, T_USES * b)
                act.activation(acc[:, :, :].rearrange("p c e -> p (c e)"), tb[0][:, :], ACT.Copy)\
                   .then_inc(t_read, 1)

            def z_silu(b, first):
                if first:
                    act.wait_ge(zn_ready, 1)
                    act.wait_ge(ld_x, 16)
                else:
                    act.wait_ge(t_full, T_USES * b)
                for c in range(TC):
                    last = act.activation(sz[:, c, :], x_sb[:, b, c, :], ACT.Silu,
                                          bias=znm[:, b, c:c + 1], scale=zrs[:, b, c:c + 1])
                last.then_inc(sz_ready, 1)

            def high_weights(k):
                if k == 0:
                    act.wait_ge(ld_ffn, 32)
                    act.activation(rhi[:, :, :], router_sb[:, :, :], ACT.Copy).then_inc(whi_ready, 1)
                act.activation(piece(whi, k), piece(raw, k), ACT.Copy).then_inc(whi_ready, 1)

            def xn_high(b, src):
                act.activation(xhi[:, :, :].rearrange("p c l -> p (c l)"), src[:, :], ACT.Copy).then_inc(xhi_ready, 1)

            def router_exp(b):
                act.wait_ge(fchain, FCHAIN * b + FVAR + 1)
                for c in range(TC):
                    last = act.activation(esc[:, c, :], sc[:, c, :], ACT.Exp, bias=smax[:, c:c + 1])
                last.then_inc(esc_ready, 1)

            def gate_silu(b, q):
                if q < NQ - 1:
                    k = f_bank(f"gate{q}")
                    act.wait_ge(f_full[k], f_count(b, f"gate{q}") + 1)
                    act.activation(gs[:, q, :], fb[k][:, :], ACT.Silu).then_inc(gs_ready, 1)
                else:
                    act.wait_ge(o_full, O_USES * b + 2)
                    act.activation(gs[:, q, :], ob[:, :], ACT.Silu).then_inc(gs_ready, 1)

            def hidden_out(b, q):
                k = f_bank(f"turn{q}")
                act.wait_ge(f_full[k], f_count(b, f"turn{q}") + 1)
                act.activation(hid_t[:, q, :], fb[k][:, :], ACT.Copy).then_inc(hidt_ready, 1)

            def body(b, slot, first, ffn, proj):
                for n in range(NS):
                    if n + DLEAD < NS:
                        decay(b, n + DLEAD, first)
                    elif proj:
                        decay(b + 1, n + DLEAD - NS, False)
                    if first and n < 4:
                        b_out(b, n + NS // 4, True)
                    if n == 0:
                        skip_term(b, first)
                    if first and 4 <= n < 4 + PIECES:
                        high_weights(n - 4)
                    if ffn and n == slot["xhi"]:
                        act.wait_ge(o_full, O_USES * (b - 1) + 1)
                        xn_high(b - 1, ob)
                    if proj and n == slot["silu"]:
                        conv_silu(b + 1, False)
                        if first:
                            z_silu(b, first)
                        act.preload_act_table_set(EXP_LN)
                    if proj and n == slot["xs"]:
                        x_proj_out(b + 1)
                    if ffn and n == slot["esc"]:
                        router_exp(b - 1)
                    if proj and n == slot["pre"]:
                        dt_out(b + 1)
                    if proj and n == slot["c_next"]:
                        c_out(b + 1, False)
                    if proj and n == slot["exp"]:
                        softplus_exp(b + 1)
                    if ffn and n == slot["gate_silu"]:
                        for q in range(NQ):
                            gate_silu(b - 1, q)
                        z_silu(b, first)
                        act.preload_act_table_set(EXP_LN)
                    if proj and n == slot["ln"]:
                        softplus_ln(b + 1)
                    for q in range(NQ):
                        if ffn and n == slot["hid_t"][q]:
                            hidden_out(b - 1, q)
                    for j in range(NS // 2):
                        if proj and n == slot["b_all"][j]:
                            b_out(b + 1, j, False)

            act.wait_ge(ld_col, 48)
            act.activation(pick[:, :], pick_f, ACT.Copy).then_inc(pick_ready, 1)
            conv_silu(0, True)
            act.activation(tg[:, :], gains_sb[:, :], ACT.Tanh).then_inc(tanh_ready, 1)
            act.preload_act_table_set(EXP_LN)
            x_proj_out(0)
            act.activation(a_exp[:, :], alog, ACT.Exp).then_inc(aexp_ready, 1)
            act.wait_ge(p_full[DT % PB], p_count(0, DT) + 1)
            for c in range(EC):
                act.activation(pre[:, c, :], p_bank(DT)[:, c * L:(c + 1) * L], ACT.Identity, bias=dtb[:, c:c + 1])\
                   .then_inc(head_act if c == 0 else p_read[DT % PB], 1)
            act.wait_ge(head_dve, 1)
            act.activation(texp[:, 0, :], texp[:, 0, :], ACT.Exp).then_inc(head_act, 1)
            act.wait_ge(pchain, 6)
            act.activation(texp[:, 1, :], texp[:, 1, :], ACT.Exp).then_inc(texp_ready, 1)
            c_out(0, True)
            act.wait_ge(head_dve, 2)
            act.activation(tln[:, 0, :], tp1[:, 0, :], ACT.Ln).then_inc(head_act, 1)
            act.wait_ge(pchain, 7)
            act.activation(tln[:, 1, :], tp1[:, 1, :], ACT.Ln).then_inc(tln_ready, 1)
            b_out(0, 0, True)
            act.wait_ge(a_ready, 2)
            act.wait_ge(head_dve, 5)
            act.activation(da[:, 0, 0, 1:L], delta[:, 0, 1:L], ACT.Exp, scale=a_neg[:, 0, 0:1])
            act.wait_ge(delta_ready, 1)
            act.activation(da[:, 0, 1, 1:L], delta[:, 1, 1:L], ACT.Exp, scale=a_neg[:, 1, 0:1]).then_inc(da_ready, 1)
            for n in range(1, DLEAD):
                if n < NS // 4:
                    b_out(0, n, True)
                decay(0, n, True)
            for j in range(DLEAD, NS // 4):
                b_out(0, j, True)
            body(0, FIRST, True, False, True)
            with act.Fori(1, B - 1) as b:
                body(b, MIDDLE, False, True, True)
            last_b = B - 1
            body(last_b, LAST, False, True, False)
            for t in range(TC):
                act.wait_ge(tail_full, T_XN + t)
                act.activation(xhi[:, :, t * P:(t + 1) * P], by_chunk(tail_xn[t]), ACT.Copy).then_inc(xhi_ready, 1)
            router_exp(last_b)
            for q in range(NQ):
                act.wait_ge(tail_full, T_GATE + q)
                act.activation(gs[:, q, :], tail_gates[q][:, :], ACT.Silu).then_inc(gs_ready, 1)
            for q in range(NQ):
                act.wait_ge(tail_full, T_TURN + q)
                act.activation(hid_t[:, q, :], tail_turns[q][:, :], ACT.Copy).then_inc(hidt_ready, 1)

        @block.vector
        def _(dve):
            def z_stats():
                for k in range(B * TC):
                    dve.bn_stats(zst[:, k, :], x_sb[:, k // TC, k % TC, :]).then_inc(zchain, 1)
                for k in range(B * TC):
                    dve.wait_ge(zchain, B * TC)
                    dve.bn_aggr(zmv[:, k, :], zst[:, k, :]).then_inc(zchain, 1)
                for k in range(B * TC):
                    dve.wait_ge(zchain, 2 * B * TC)
                    dve.tensor_scalar(zve[:, k:k + 1], zmv[:, k, 1:2], EPS, None, ALU.add).then_inc(zchain, 1)

            dve.memset(da[:, :, :, 0:1], 0.0).then_inc(a_ready, 1)

            dve.wait_ge(ld_in, 32)
            for c in range(EC):
                cols_c = slice(c * P, (c + 1) * P)
                dve.tensor_tensor(wk_sb[:, :, cols_c], convw_sb[:, :, cols_c],
                                  win_sb[:, cols_c].unsqueeze(1).to_broadcast([P, TAPS, P]), ALU.mult).then_inc(wk_made, 1)
                dve.wait_ge(wk_made, c + 1)
                dve.tensor_copy(wk_hi[:, :, cols_c], wk_sb[:, :, cols_c]).then_inc(wk_ready, 1)
                dve.wait_ge(wk_ready, 2 * c + 1)
                dve.tensor_tensor(wk_lo[:, :, cols_c], wk_sb[:, :, cols_c], wk_hi[:, :, cols_c].bitcast(fp32),
                                  ALU.subtract).then_inc(wk_ready, 1)
            dve.wait_ge(ld_x, 16)
            z_stats()
            dve.wait_ge(aexp_ready, 1)
            dve.tensor_scalar(a_neg[:, :, :].rearrange("p c n -> p (c n)"), a_exp[:, :], -1.0, None, ALU.mult)\
               .then_inc(a_ready, 1)

            def z_shift():
                dve.wait_ge(zrs_ready, 1)
                dve.scalar_tensor_tensor(znm[:, :, :].rearrange("p b c -> p (b c)"), zmv[:, :, 0], -1.0,
                                         zrs[:, :, :].rearrange("p b c -> p (b c)"), ALU.mult, ALU.mult)\
                   .then_inc(zn_ready, 1)

            def split_b(b):
                k = PCHAIN * b
                dve.wait_ge(high_ready, b + 1)
                dve.tensor_tensor(rest1[:, :], xs[0:DT0, :], part3[:, :], ALU.subtract).then_inc(pchain, 1)
                dve.wait_ge(pchain, k + 1)
                dve.tensor_copy(mid64[:, :], rest1[:, :]).then_inc(pchain, 1)
                dve.wait_ge(pchain, k + 2)
                dve.tensor_tensor(rest2[:, :], rest1[:, :], mid64[:, :], ALU.subtract).then_inc(pchain, 1)
                dve.tensor_copy(part3[32:64, :], mid64[32:64, :]).then_inc(pchain, 1)
                dve.wait_ge(pchain, k + 3)
                dve.tensor_copy(part3[64:96, :], rest2[64:96, :]).then_inc(pchain, 1)

            def softplus_abs(b):
                dve.wait_ge(p_read[DT % PB], p_count(b, DT) + 1)
                dve.scalar_tensor_tensor(flat(texp), flat(pre), -1.0, flat(pre), ALU.mult, ALU.min)\
                   .then_inc(pchain, 1)

            def softplus_one(b):
                dve.wait_ge(texp_ready, b + 1)
                dve.tensor_scalar(flat(tp1), flat(texp), 1.0, None, ALU.add).then_inc(pchain, 1)

            def softplus_fix(b, first):
                if not first:
                    dve.wait_ge(delta_ready, b)
                dve.wait_ge(pchain, PCHAIN * b + 7)
                dve.scalar_tensor_tensor(flat(nfix), flat(tp1), -1.0, flat(texp), ALU.add, ALU.subtract)\
                   .then_inc(pchain, 1)

            def softplus_sum(b):
                dve.wait_ge(tln_ready, b + 1)
                dve.scalar_tensor_tensor(flat(sp), flat(pre), 0.0, flat(tln), ALU.max, ALU.add).then_inc(pchain, 1)

            def flat(t):
                return t[:, :, :].rearrange("p c l -> p (c l)")

            def take_du(b, first):
                dve.wait_ge(delta_ready, b + 1)
                dve.wait_ge(p_read[IN], p_count(b, IN) + 1)
                if not first:
                    dve.wait_ge(dbu_ready, NS * b)
                dve.tensor_tensor(flat(du), flat(delta), flat(u), ALU.mult).then_inc(du_ready, 1)

            def take_c(b):
                dve.wait_ge(p_read[CP % PB], p_count(b, CP) + 1)
                dve.tensor_copy(c_t[:, :, :], c_next[:, :, :]).then_inc(c_ready, 1)

            def scan(b, n, first):
                dve.wait_ge(da_ready, NS * b + n + 1)
                dve.wait_ge(dbu_ready, NS * b + n + 1)
                if n >= HR:
                    dve.wait_ge(t_full, T_USES * b + n - HR + 2)
                elif not first:
                    dve.wait_ge(t_full, T_USES * (b - 1) + NS + n - HR + 2)
                dve.tensor_tensor_scan(h[:, n % HR, :, :].rearrange("p c l -> p (c l)"), da[:, n % DA, :, :].rearrange("p c l -> p (c l)"),
                                       dbu[:, n % RING, :, :].rearrange("p c l -> p (c l)"), 0.0,
                                       ALU.mult, ALU.add).then_inc(scan_done, 1)

            def add_state(b, n):
                dve.wait_ge(t_full, T_USES * b + n + 2)
                dve.wait_ge(t_read, T_USES * b + n + 1)
                if n == 0:
                    dve.wait_ge(c_ready, b + 1)
                src = tb[(n + 1) % 2]
                for c in range(TC):
                    last = dve.scalar_tensor_tensor(acc[:, c, :], src[:, c * DI:(c + 1) * DI], c_t[:, c, n:n + 1],
                                                    acc[:, c, :], ALU.mult, ALU.add)
                last.then_inc(t_read, 1)

            def gate_y(b):
                dve.wait_ge(t_full, T_USES * (b + 1))
                dve.wait_ge(t_read, T_USES * (b + 1) - 1)
                dve.tensor_tensor(flat(yg), tb[(NS + 1) % 2][:, :], flat(acc), ALU.mult).then_inc(t_read, 1)
                dve.wait_ge(t_read, T_USES * (b + 1))
                row = x_sb[:, b, :, :].rearrange("p c e -> p (c e)")
                dve.scalar_tensor_tensor(row, flat(yg), tg[:, 0:1], row, ALU.mult, ALU.add)\
                   .then_inc(x1_ready, 1)

            def row_stats(b, last):
                k = FCHAIN * b
                dve.wait_ge(x1_ready, b + 1)
                for c in range(TC):
                    dve.bn_stats(fst[:, c, :], x_sb[:, b, c, :]).then_inc(fchain, 1)
                dve.wait_ge(fchain, k + TC)
                if not last:
                    take_c(b + 1)
                for c in range(TC):
                    dve.bn_aggr(fmv[:, c, :], fst[:, c, :]).then_inc(fchain, 1)
                dve.wait_ge(fchain, k + 2 * TC)
                dve.tensor_scalar(fve[:, :], fmv[:, :, 1], EPS, None, ALU.add).then_inc(fchain, 1)

            def normalise(b):
                dve.wait_ge(frs_ready, b + 1)
                for c in range(TC):
                    last = dve.tensor_scalar(xn[:, c, :], x_sb[:, b, c, :], fmv[:, c, 0:1], frs[:, c:c + 1],
                                             ALU.subtract, ALU.mult)
                last.then_inc(xn_ready, 1)

            def xn_low(b, src):
                dve.wait_ge(xhi_ready, b + 1)
                dve.tensor_tensor(flat(xlo), src[:, :], flat(xhi).bitcast(fp32), ALU.subtract).then_inc(o_read, 1)

            def low_router():
                dve.wait_ge(whi_ready, 1)
                dve.tensor_tensor(rlo[:, :, :], router_sb[:, :, :], rhi[:, :, :].bitcast(fp32), ALU.subtract)\
                   .then_inc(wlo_ready, 1)

            def router_max(b):
                k = f_bank("scores")
                dve.wait_ge(f_full[k], f_count(b, "scores") + 1)
                dve.tensor_copy(sc[:, :, :].rearrange("p c e -> p (c e)"), fb[k][:, 0:TC * NE]).then_inc(sc_read, 1)
                dve.wait_ge(sc_read, b + 1)
                dve.tensor_reduce(smax[:, :], sc[:, :, :], mybir.AxisListType.X, ALU.max, negate=True)\
                   .then_inc(fchain, 1)

            def router_weights(b):
                k = FCHAIN * b + FVAR + 1
                for c in range(TC):
                    dve.max(top[:, c, :], esc[:, c, :]).then_inc(fchain, 1)
                dve.wait_ge(fchain, k + TC)
                dve.tensor_tensor(tsum[:, :], top[:, :, 0], top[:, :, 1], ALU.add)
                for c in range(TC):
                    last = dve.max_index(topi[:, c, :], top[:, c, :], esc[:, c, :])
                last.then_inc(fchain, 1)
                dve.wait_ge(fchain, k + TC + 1)
                dve.tensor_copy(topf[:, :, 0:2], topi[:, :, 0:2]).then_inc(fchain, 1)
                dve.reciprocal(trec[:, :], tsum[:, :])
                dve.wait_ge(fchain, k + TC + 2)
                for c in range(TC):
                    last = dve.tensor_scalar(hot1[:, c, :], iota, topf[:, c, 0:1], None, ALU.is_equal)
                last.then_inc(fchain, 1)
                dve.wait_ge(fchain, k + TC + 3)
                for c in range(TC):
                    last = dve.scalar_tensor_tensor(hot2[:, c, :], iota, topf[:, c, 1:2], hot1[:, c, :],
                                                    ALU.is_equal, ALU.add)
                last.then_inc(fchain, 1)
                dve.wait_ge(fchain, k + TC + 4)
                for c in range(TC):
                    last = dve.scalar_tensor_tensor(wt[:, c, :], esc[:, c, :], trec[:, c:c + 1], hot2[:, c, :],
                                                    ALU.mult, ALU.mult)
                last.then_inc(w_ready, 1)

            def hidden(b, q):
                dve.wait_ge(gw_ready, NQ * b + q + 1)
                if q < PB:
                    dve.wait_ge(early_full, PB * b + q + 1)
                    src = pb[q]
                else:
                    k = f_bank(f"up{q}")
                    dve.wait_ge(f_full[k], f_count(b, f"up{q}") + 1)
                    src = fb[k]
                dve.tensor_tensor(gs[:, q, :], src[:, :], gs[:, q, :], ALU.mult).then_inc(hid_ready, 1)

            def weigh_direct(b, q):
                dve.wait_ge(gs_ready, NQ * b + q + 1)
                dve.tensor_tensor(by_expert(gs, q), by_expert(gs, q), weights_of(q), ALU.mult).then_inc(gw_ready, 1)

            def hidden_direct(b, q):
                dve.wait_ge(gw_ready, NQ * b + q + 1)
                dve.wait_ge(tail_full, T_UP + q)
                dve.tensor_tensor(gs[:, q, :], tail_ups[q][:, :], gs[:, q, :], ALU.mult).then_inc(hid_ready, 1)

            def finish(b):
                row = x_sb[:, b, :, :].rearrange("p c e -> p (c e)")
                dve.wait_ge(o_full, O_USES * (b + 1))
                dve.scalar_tensor_tensor(row, ob[:, :], tg[:, 1:2], row, ALU.mult, ALU.add).then_inc(out_ready, 1)

            def body(b, slot, first, ffn, proj):
                for n in range(NS):
                    if n + AHEAD < NS:
                        scan(b, n + AHEAD, first)
                    elif proj:
                        scan(b + 1, n + AHEAD - NS, False)
                    if ffn and n == 0:
                        row_stats(b - 1, False)
                    if ffn and n == slot["top"]:
                        dve.wait_ge(esc_ready, b)
                    add_state(b, n)
                    if first and n == 5:
                        low_router()
                    if ffn and n == slot["xn"]:
                        normalise(b - 1)
                    if ffn and n == slot["xlo"]:
                        xn_low(b - 1, ob)
                    if ffn and n == slot["smax"]:
                        router_max(b - 1)
                    if ffn and n == slot["top"]:
                        router_weights(b - 1)
                    if proj and n == slot["split"]:
                        split_b(b + 1)
                    if proj and n == slot["neg"]:
                        softplus_abs(b + 1)
                    if proj and n == slot["one"]:
                        softplus_one(b + 1)
                        softplus_fix(b + 1, False)
                    for q in range(NQ):
                        if ffn and n == slot["hid"][q]:
                            hidden(b - 1, q)
                    if proj and n == slot["sum"]:
                        softplus_sum(b + 1)
                    if proj and n == slot["du"]:
                        take_du(b + 1, False)
                gate_y(b)
                if ffn and proj:
                    finish(b - 1)

            split_b(0)
            dve.wait_ge(head_act, 1)
            dve.scalar_tensor_tensor(texp[:, 0, :], pre[:, 0, :], -1.0, pre[:, 0, :], ALU.mult, ALU.min).then_inc(head_dve, 1)
            dve.wait_ge(p_read[DT % PB], p_count(0, DT) + 1)
            dve.scalar_tensor_tensor(texp[:, 1, :], pre[:, 1, :], -1.0, pre[:, 1, :], ALU.mult, ALU.min).then_inc(pchain, 1)
            dve.wait_ge(head_act, 2)
            dve.tensor_scalar(tp1[:, 0, :], texp[:, 0, :], 1.0, None, ALU.add).then_inc(head_dve, 1)
            dve.wait_ge(texp_ready, 1)
            dve.tensor_scalar(tp1[:, 1, :], texp[:, 1, :], 1.0, None, ALU.add).then_inc(pchain, 1)
            dve.wait_ge(head_dve, 2)
            dve.scalar_tensor_tensor(nfix[:, 0, :], tp1[:, 0, :], -1.0, texp[:, 0, :], ALU.add, ALU.subtract)\
               .then_inc(head_dve, 1)
            dve.wait_ge(pchain, 7)
            dve.scalar_tensor_tensor(nfix[:, 1, :], tp1[:, 1, :], -1.0, texp[:, 1, :], ALU.add, ALU.subtract)\
               .then_inc(pchain, 1)
            dve.wait_ge(head_act, 3)
            dve.scalar_tensor_tensor(sp[:, 0, :], pre[:, 0, :], 0.0, tln[:, 0, :], ALU.max, ALU.add).then_inc(head_dve, 1)
            dve.wait_ge(tln_ready, 1)
            dve.scalar_tensor_tensor(sp[:, 1, :], pre[:, 1, :], 0.0, tln[:, 1, :], ALU.max, ALU.add).then_inc(pchain, 1)
            dve.wait_ge(head_dve, 4)
            dve.tensor_tensor(delta[:, 0, :], sp[:, 0, :], nfix[:, 0, :], ALU.subtract).then_inc(head_dve, 1)
            dve.wait_ge(pchain, 9)
            dve.tensor_tensor(delta[:, 1, :], sp[:, 1, :], nfix[:, 1, :], ALU.subtract).then_inc(delta_ready, 1)
            dve.wait_ge(head_dve, 5)
            dve.tensor_tensor(du[:, 0, :], delta[:, 0, :], u[:, 0, :], ALU.mult).then_inc(head_dve, 1)
            dve.wait_ge(delta_ready, 1)
            dve.tensor_tensor(du[:, 1, :], delta[:, 1, :], u[:, 1, :], ALU.mult).then_inc(du_ready, 1)
            take_c(0)
            z_shift()
            dve.wait_ge(tanh_ready, 1)
            for n in range(AHEAD):
                scan(0, n, True)
            body(0, FIRST, True, False, True)
            with dve.Fori(1, B - 1) as b:
                body(b, MIDDLE, False, True, True)
            body(B - 1, LAST, False, True, False)
            last_b = B - 1
            row_stats(last_b, True)
            dve.wait_ge(frs_ready, B)
            for t in range(TC):
                dve.tensor_scalar(xn[:, t, :], x_sb[:, last_b, t, :], fmv[:, t, 0:1], frs[:, t:t + 1],
                                  ALU.subtract, ALU.mult).then_inc(xn_ready, 1)
            for t in range(TC):
                dve.wait_ge(xhi_ready, B + t)
                dve.tensor_tensor(xlo[:, :, t * P:(t + 1) * P], by_chunk(tail_xn[t]),
                                  xhi[:, :, t * P:(t + 1) * P].bitcast(fp32), ALU.subtract).then_inc(o_read, 1)
            finish(last_b - 1)
            router_max(last_b)
            dve.wait_ge(esc_ready, B)
            router_weights(last_b)
            dve.wait_ge(w_ready, B)
            for q in range(NQ):
                weigh_direct(last_b, q)
            for q in range(NQ):
                hidden_direct(last_b, q)
            for t in range(TC):
                dve.wait_ge(o_full, O_USES * last_b + t + 1)
                dve.scalar_tensor_tensor(x_sb[:, last_b, t, :], tail_sums[t][:, t * DI:(t + 1) * DI], tg[:, 1:2],
                                         x_sb[:, last_b, t, :], ALU.mult, ALU.add).then_inc(out_ready, 1)

        @block.tensor
        def _(pe):
            def in_proj(b, c, first):
                if first:
                    pe.wait_ge(ctx_ready, 1)
                    pe.wait_ge(wk_ready, 2 * c + 1)
                elif c == 0:
                    pe.wait_ge(p_read[IN], p_count(b, IN))
                dst = p_bank(IN)[:, c * L:(c + 1) * L]
                for wk, part in ((wk_hi, ctx_hi), (wk_hi, ctx_lo), (wk_lo, ctx_hi)):
                    for k in range(TAPS):
                        if first and wk is wk_lo and k == 0:
                            pe.wait_ge(wk_ready, 2 * c + 2)
                        last = pe.matmul(dst, wk[:, k, c * P:(c + 1) * P], part[:, b, k:k + L],
                                         start=(wk is wk_hi and part is ctx_hi and k == 0),
                                         stop=(wk is wk_lo and k == TAPS - 1))
                if c == EC - 1:
                    last.then_inc(p_full[IN], 1)

            def x_proj(b, first):
                pe.wait_ge(p_read[IN], p_count(b, IN) + 1)
                if first:
                    pe.wait_ge(ld_wx, 32)
                else:
                    pe.wait_ge(p_read[XP % PB], p_count(b, XP))
                for c in range(EC):
                    last = pe.matmul(p_bank(XP)[0:XW, 0:L], wx_sb[:, c, 0:XW], u[:, c, :], start=(c == 0),
                                     stop=(c == EC - 1))
                last.then_inc(p_full[XP % PB], 1)

            def dt_proj(b):
                pe.wait_ge(p_read[XP % PB], p_count(b, XP) + 1)
                pe.wait_ge(p_read[DT % PB], p_count(b, DT))
                for c in range(EC):
                    last = pe.matmul(p_bank(DT)[:, c * L:(c + 1) * L], wdt_sb[DT0:C0, c * P:(c + 1) * P],
                                     xs[DT0:C0, :], start=True, stop=True)
                last.then_inc(p_full[DT % PB], 1)

            def c_proj(b):
                for t in range(TC):
                    last = pe.transpose(p_bank(CP)[:, t * (XW - DT0):(t + 1) * (XW - DT0)],
                                        xs[DT0:XW, t * P:(t + 1) * P], ident[DT0:XW, DT0:XW])
                last.then_inc(p_full[CP % PB], 1)

            def b_spread(b, j, first):
                if j == 0:
                    pe.wait_ge(pchain, PCHAIN * b + 5)
                    if first:
                        pe.wait_ge(pick_ready, 1)
                k = BP + j
                pe.wait_ge(p_read[k % PB], p_count(b, k))
                for i in range(2):
                    n = 2 * j + i
                    last = pe.matmul(p_bank(k)[:, i * L:(i + 1) * L], pick[:, n:n + 1].to_broadcast([DT0, P]),
                                     part3[:, :], start=True, stop=True)
                last.then_inc(p_full[k % PB], 1)

            def skip_term(b, first):
                if first:
                    pe.wait_ge(ld_col, 48)
                else:
                    pe.wait_ge(t_read, T_USES * b - 1)
                pe.wait_ge(ud_ready, b + 1)
                for t in range(TC):
                    for c in range(EC):
                        o = t * DI + c * P
                        last = pe.transpose(tb[0][:, o:o + P], ud[:, c, t * P:(t + 1) * P], ident)
                last.then_inc(t_full, 1)

            def turn_state(b, n, first):
                pe.wait_ge(scan_done, NS * b + n + 1)
                if n >= 1:
                    pe.wait_ge(t_read, T_USES * b + n)
                elif not first:
                    pe.wait_ge(t_read, T_USES * b)
                for t in range(TC):
                    for c in range(EC):
                        o = t * DI + c * P
                        last = pe.transpose(tb[(n + 1) % 2][:, o:o + P], h[:, n % HR, c, t * P:(t + 1) * P], ident)
                last.then_inc(t_full, 1)

            def turn_z(b):
                pe.wait_ge(sz_ready, b + 1)
                pe.wait_ge(t_read, T_USES * b + NS)
                for t in range(TC):
                    for c in range(EC):
                        o = t * DI + c * P
                        last = pe.transpose(tb[(NS + 1) % 2][:, o:o + P], sz[:, c, t * P:(t + 1) * P], ident)
                last.then_inc(t_full, 1)

            def turn_xn(b, dst):
                pe.wait_ge(xn_ready, b + 1)
                for c in range(EC):
                    for t in range(TC):
                        last = pe.transpose(dst[:, c * L + t * P:c * L + (t + 1) * P], xn[:, t, c * P:(c + 1) * P], ident)
                return last

            def three(out_ap, t, hi, lo, c):
                xh, xl = xhi[:, c, t * P:(t + 1) * P], xlo[:, c, t * P:(t + 1) * P]
                pe.matmul(out_ap, xh, hi, start=(c == 0), stop=False)
                pe.matmul(out_ap, xh, lo, start=False, stop=False)
                return pe.matmul(out_ap, xl, hi, start=False, stop=(c == EC - 1))

            def router(b):
                pe.wait_ge(xhi_ready, b + 1)
                pe.wait_ge(o_read, O_READS * b + 1)
                scores(b)

            def scores(b):
                k = f_bank("scores")
                for t in range(TC):
                    for c in range(EC):
                        last = three(fb[k][:, t * NE:(t + 1) * NE], t, rhi[:, c, :], rlo[:, c, :], c)
                last.then_inc(f_full[k], 1)

            def quarter(dst, q, what):
                t, half = q // HALVES, q % HALVES
                for c in range(EC):
                    k = (c * 2 + what) * HALVES + half
                    last = three(dst[:, :], t, piece(whi, k).rearrange("p e f -> p (e f)"),
                                 piece(wlo, k).rearrange("p e f -> p (e f)"), c)
                return last

            def gates(b, q):
                if q < NQ - 1:
                    k = f_bank(f"gate{q}")
                    if q == 2:
                        pe.wait_ge(sc_read, b + 1)
                    quarter(fb[k], q, 0).then_inc(f_full[k], 1)
                else:
                    quarter(ob, q, 0).then_inc(o_full, 1)

            def ups(b, q, proj):
                if q < PB:
                    pe.wait_ge(p_read[q], P_USES * (b + 2) + (CP // PB + 1 if proj else 0))
                    quarter(pb[q], q, 1).then_inc(early_full, 1)
                else:
                    k = f_bank(f"up{q}")
                    pe.wait_ge(gs_ready, NQ * b + q - 1)
                    quarter(fb[k], q, 1).then_inc(f_full[k], 1)

            def turn(dst, q):
                for e in range(QE):
                    last = pe.transpose(dst[:, e * P:(e + 1) * P], gs[:, q, e * F:(e + 1) * F], ident)
                return last

            def turn_hidden(b, q):
                k = f_bank(f"turn{q}")
                pe.wait_ge(hid_ready, NQ * b + q + 1)
                if q == 0:
                    pe.wait_ge(gs_ready, NQ * b + 3)
                elif q == 1:
                    pe.wait_ge(hidt_ready, NQ * b + 1)
                turn(fb[k], q).then_inc(f_full[k], 1)

            def downs(dst, q, experts=range(QE)):
                t, half = q // HALVES, q % HALVES
                for e in experts:
                    last = pe.matmul(dst[:, t * DI:(t + 1) * DI], hid_t[:, q, e * P:(e + 1) * P],
                                     down_sb[:, half * QE + e, :], start=(half == 0 and e == 0),
                                     stop=(half == HALVES - 1 and e == QE - 1))
                return last

            def downs_of(b, k):
                q = k // 2
                if k == 0:
                    pe.wait_ge(gs_ready, NQ * (b + 1))
                if k % 2 == 0:
                    pe.wait_ge(hidt_ready, NQ * b + q + 1)
                last = downs(ob, q, range(k % 2 * QE // 2, (k % 2 + 1) * QE // 2))
                if k == 2 * NQ - 1:
                    last.then_inc(o_full, 1)

            def body(b, slot, first, ffn, proj):
                for n in range(-1, NS + 1):
                    if n == NS:
                        turn_z(b)
                    elif n >= 0:
                        turn_state(b, n, first)
                    if first and 0 <= n < NS // 4:
                        b_spread(b, n + NS // 4, True)
                    for c in range(EC):
                        if proj and n == slot["in"][c]:
                            in_proj(b + 1, c, False)
                    if ffn and n == slot["turn_xn"]:
                        turn_xn(b - 1, ob).then_inc(o_full, 1)
                    if ffn and n == slot["router"]:
                        router(b - 1)
                    if proj and n == slot["x_proj"]:
                        x_proj(b + 1, False)
                    if proj and n == slot["dt"]:
                        dt_proj(b + 1)
                        c_proj(b + 1)
                    for q in range(NQ):
                        if ffn and n == slot["gate"][q]:
                            gates(b - 1, q)
                    for q in range(NQ):
                        if ffn and n == slot["up"][q]:
                            ups(b - 1, q, proj)
                    for q in range(NQ):
                        if ffn and n == slot["turn"][q]:
                            turn_hidden(b - 1, q)
                    for k in range(2 * NQ):
                        if ffn and n == slot["down"][k]:
                            downs_of(b - 1, k)
                    for j in range(NS // 2):
                        if proj and n == slot["b"][j]:
                            if ffn and j < PB:
                                pe.wait_ge(hid_ready, NQ * (b - 1) + j + 1)
                            b_spread(b + 1, j, False)
                if proj:
                    skip_term(b + 1, False)

            in_proj(0, 0, True)
            in_proj(0, 1, True)
            x_proj(0, True)
            dt_proj(0)
            c_proj(0)
            for j in range(NS // 4):
                b_spread(0, j, True)
            skip_term(0, True)
            pe.wait_ge(ctx_ready, 2)
            body(0, FIRST, True, False, True)
            pe.wait_ge(wlo_ready, PIECES + 1)
            pe.wait_ge(ld_down, 16)
            with pe.Fori(1, B - 1) as b:
                body(b, MIDDLE, False, True, True)
            last_b = B - 1
            body(last_b, LAST, False, True, False)
            for t in range(TC):
                pe.wait_ge(xn_ready, B + t)
                for c in range(EC):
                    last = pe.transpose(tail_xn[t][:, c * P:(c + 1) * P], xn[:, t, c * P:(c + 1) * P], ident)
                last.then_inc(tail_full, 1)
            for q in range(NQ):
                if q % HALVES == 0:
                    t = q // HALVES
                    pe.wait_ge(xhi_ready, B + t)
                    pe.wait_ge(o_read, O_READS * last_b + t + 1)
                    if t == TC - 1:
                        scores(last_b)
                quarter(tail_gates[q], q, 0).then_inc(tail_full, 1)
            for q in range(NQ):
                if q == 2:
                    pe.wait_ge(sc_read, B)
                elif q == 3:
                    pe.wait_ge(gs_ready, NQ * last_b + 1)
                quarter(tail_ups[q], q, 1).then_inc(tail_full, 1)
            for q in range(NQ):
                pe.wait_ge(hid_ready, NQ * last_b + q + 1)
                if q < NQ - 1:
                    pe.wait_ge(gs_ready, NQ * last_b + q + 2)
                turn(tail_turns[q], q).then_inc(tail_full, 1)
                if q == 1:
                    pe.wait_ge(out_ready, B - 1)
                if q >= 1:
                    pe.wait_ge(hidt_ready, NQ * last_b + q)
                    last = downs(tail_sums[(q - 1) // HALVES], q - 1)
                    if q % HALVES == 0:
                        last.then_inc(o_full, 1)
            pe.wait_ge(hidt_ready, NQ * B)
            downs(tail_sums[TC - 1], NQ - 1).then_inc(o_full, 1)


def kernel(x, ctx_1024, g_xattn, g_ffn, L0_xattn_in_proj_w, L0_xattn_conv_w, L0_xattn_conv_b, L0_xattn_x_proj_w,
           L0_xattn_dt_proj_w, L0_xattn_dt_proj_b, L0_xattn_A_log, L0_xattn_D, L0_ffn_router_w, L0_ffn_gate_proj,
           L0_ffn_up_proj, L0_ffn_down_proj):
    import numpy as np
    import concourse.bacc as bacc
    from concourse.bass_utils import run_bass_kernel_spmd

    P = 128

    def arr(a):
        return np.asarray(a)

    def by_partition(a):
        a = arr(a)
        return np.swapaxes(a.reshape((a.shape[0] // P, P) + a.shape[1:]), 0, 1)

    xw = arr(L0_xattn_x_proj_w)
    ns = arr(L0_xattn_A_log).shape[1]
    dr = arr(L0_xattn_dt_proj_w).shape[1]
    dt_rows, b_rows, c_rows = xw[:dr], xw[dr:dr + ns], xw[dr + ns:]
    gap = np.zeros((32 - ns, xw.shape[1]), xw.dtype)
    w_x = np.concatenate([b_rows, gap, b_rows, gap, b_rows, gap, dt_rows, c_rows], 0).T
    ne = arr(L0_ffn_router_w).shape[1]
    consts = np.zeros((P, P + 32 + ne + 1), np.float32)
    consts[:, :P] = np.eye(P)
    consts[:, P:P + 32] = np.tile(np.eye(32), (P // 32, 1))
    consts[:, P + 32:P + 32 + ne] = np.arange(ne)
    consts[:, P + 32 + ne] = -0.5
    data = {
        "x": arr(x),
        "ctx_t": np.transpose(arr(ctx_1024), (2, 0, 1)),
        "w_in_t": arr(L0_xattn_in_proj_w).T,
        "conv_w_t": arr(L0_xattn_conv_w).T.reshape(-1),
        "cols": np.concatenate([by_partition(L0_xattn_conv_b), by_partition(L0_xattn_dt_proj_b),
                                by_partition(L0_xattn_D), by_partition(L0_xattn_A_log).reshape(P, -1)], 1),
        "w_x": by_partition(w_x),
        "w_dt_t": arr(L0_xattn_dt_proj_w).T,
        "w_router": by_partition(L0_ffn_router_w),
        "w_gate_up": np.transpose(np.stack([arr(L0_ffn_gate_proj), arr(L0_ffn_up_proj)], 1)
                                  .reshape(ne, 2, -1, P, P), (3, 2, 1, 0, 4)),
        "w_down": np.transpose(arr(L0_ffn_down_proj), (1, 0, 2)),
        "gains": np.concatenate([arr(g_xattn), arr(g_ffn)]),
        "consts": consts,
    }
    nc = bacc.Bacc("TRN2", target_bir_lowering=False, num_devices=1)
    arrays, args = {}, {}
    for name, a in data.items():
        a = np.ascontiguousarray(a)
        arrays[f"in_{name}"] = a
        args[name] = nc.dram_tensor(f"in_{name}", a.shape, mybir.dt.from_np(a.dtype), kind="ExternalInput").ap()
    out = nc.dram_tensor("out", data["x"].shape, mybir.dt.float32, kind="ExternalOutput").ap()
    mamba_moe_program(nc, out=out, **args)
    r = run_bass_kernel_spmd(nc, [arrays], core_ids=[0])
    return r.results[0]["out"]
```
